# Optimizing a Trainium2 kernel written in Bass

```python
import numpy as np
import jax
import jax.numpy as jnp

def _softmax(x, axis=-1):
    return jax.nn.softmax(x, axis=axis)

def _gelu(x):
    return jax.nn.gelu(x, approximate=True)

def _silu(x):
    return jax.nn.silu(x)

def _sigmoid(x):
    return jax.nn.sigmoid(x)

def _layernorm(x, axis=-1, eps=1e-05):
    m = jnp.mean(x, axis=axis, keepdims=True)
    v = jnp.var(x, axis=axis, keepdims=True)
    return (x - m) / jnp.sqrt(v + eps)

def _scatter_add(tgt, idx, src, axis=0):
    return tgt.at[idx].add(src)

def _segment_sum(src, seg, n):
    return jax.ops.segment_sum(src, seg, n)
kernel_name = 'mk_hybrid_d1_jaxref_r4_de6e15'

def setup_inputs(seed: int=0):
    np.random.seed(seed)
    _w = jnp.asarray

    def _L0_attn_a_setup():
        import jax, jax.numpy as jnp
        import numpy as np
        N_EMBED = 256
        D_STATE = 16
        D_CONV = 4
        DT_RANK = 64
        BATCH, SEQ = (4, 512)

        def layernorm(x, g, b, eps=1e-05):
            mu = jnp.mean(x, -1, keepdims=True)
            var = jnp.mean((x - mu) ** 2, -1, keepdims=True)
            return (x - mu) * jax.lax.rsqrt(var + eps) * g + b

        def rmsnorm(x, w, eps=1e-05):
            return x * jax.lax.rsqrt(jnp.mean(x * x, -1, keepdims=True) + eps) * w

        def mamba_mixer(x, in_proj_w, conv_w, conv_b, x_proj_w, dt_proj_w, dt_proj_b, A_log, D_param, out_proj_w):
            Bt, L, D = x.shape
            ED = in_proj_w.shape[1] // 2
            N = A_log.shape[1]
            K = conv_w.shape[-1]
            xz = x @ in_proj_w
            xi, z = jnp.split(xz, 2, axis=-1)
            xc = jnp.swapaxes(xi, 1, 2)
            xc = jax.lax.conv_general_dilated(xc, conv_w[:, None, :], window_strides=(1,), padding=[(K - 1, 0)], feature_group_count=ED, dimension_numbers=('NCH', 'OIH', 'NCH'))
            xc = jnp.swapaxes(xc + conv_b[None, :, None], 1, 2)
            xc = jax.nn.silu(xc)
            dbc = xc @ x_proj_w
            dt_rank = dt_proj_w.shape[0]
            delta = jax.nn.softplus(dbc[..., :dt_rank] @ dt_proj_w + dt_proj_b)
            Bm = dbc[..., dt_rank:dt_rank + N]
            Cm = dbc[..., dt_rank + N:]
            A = -jnp.exp(A_log)
            deltaA = jnp.exp(delta[..., None] * A)
            BX = (delta * xc)[..., None] * Bm[:, :, None, :]

            def step(h, inp):
                dA, bx, c = inp
                h = dA * h + bx
                return (h, jnp.einsum('ben,bn->be', h, c))
            h0 = jnp.zeros((Bt, ED, N), x.dtype)
            _, ys = jax.lax.scan(step, h0, (jnp.swapaxes(deltaA, 0, 1), jnp.swapaxes(BX, 0, 1), jnp.swapaxes(Cm, 0, 1)))
            y = jnp.swapaxes(ys, 0, 1) + D_param * xc
            y = y * jax.nn.silu(z)
            return y @ out_proj_w
        key = jax.random.key(seed)
        ks = jax.random.split(key, 12)
        D, ED, N, K, R = (N_EMBED, N_EMBED, D_STATE, D_CONV, DT_RANK)
        s = 0.02
        inp = {'x': jax.random.normal(ks[0], (BATCH, SEQ, D), jnp.float32), 'ln1_g': jnp.ones((D,), jnp.float32), 'ln1_b': jnp.zeros((D,), jnp.float32), 'ln2_g': jnp.ones((D,), jnp.float32), 'ln2_b': jnp.zeros((D,), jnp.float32), 'rms_w': jnp.ones((D,), jnp.float32), 'in_proj_w': jax.random.normal(ks[1], (D, 2 * ED), jnp.float32) * s, 'conv_w': jax.random.normal(ks[2], (ED, K), jnp.float32) * 0.3, 'conv_b': jnp.zeros((ED,), jnp.float32), 'x_proj_w': jax.random.normal(ks[3], (ED, R + 2 * N), jnp.float32) * s, 'dt_proj_w': jax.random.normal(ks[4], (R, ED), jnp.float32) * R ** (-0.5), 'dt_proj_b': jnp.log(jnp.expm1(jnp.full((ED,), 0.01, jnp.float32))), 'A_log': jnp.log(jnp.broadcast_to(jnp.arange(1, N + 1, dtype=jnp.float32), (ED, N))), 'D_param': jnp.ones((ED,), jnp.float32), 'out_proj_w': jax.random.normal(ks[5], (ED, D), jnp.float32) * s, 'ffn_w1': jax.random.normal(ks[6], (D, 4 * D), jnp.float32) * s, 'ffn_b1': jnp.zeros((4 * D,), jnp.float32), 'ffn_w2': jax.random.normal(ks[7], (4 * D, D), jnp.float32) * s, 'ffn_b2': jnp.zeros((D,), jnp.float32)}
        return inp
    _L0_attn_a_in = _L0_attn_a_setup()

    def _L0_attn_b_setup():
        import jax, jax.numpy as jnp
        import numpy as np
        B, T, E, H = (2, 512, 256, 16)
        D = E // H
        key = jax.random.key(seed)
        k = jax.random.split(key, 6)
        return {'x': jax.random.normal(k[0], (B, T, E), dtype=jnp.float32), 'w_att_val': jax.random.normal(k[1], (H, D, D), dtype=jnp.float32) * (6.0 / D) ** 0.5, 'wv_w': jax.random.normal(k[2], (E, E), dtype=jnp.float32) * E ** (-0.5), 'wv_b': jnp.zeros((E,), dtype=jnp.float32), 'out_w': jax.random.normal(k[3], (E, E), dtype=jnp.float32) * E ** (-0.5), 'out_b': jnp.zeros((E,), dtype=jnp.float32)}
    _L0_attn_b_in = _L0_attn_b_setup()

    def _L0_ffn_setup():
        import jax, jax.numpy as jnp
        import numpy as np
        from jax import lax
        T, B, I, M, O = (64, 64, 256, 256, 256)

        def _xavier(key, shape):
            fan_out, fan_in = shape
            limit = float(np.sqrt(6.0 / (fan_in + fan_out)))
            return jax.random.uniform(key, shape, jnp.float32, -limit, limit)
        key = jax.random.key(seed)
        ks = jax.random.split(key, 9)
        x = jax.random.normal(ks[0], (T, B, I), jnp.float32)
        return {'x': x, 'wf': _xavier(ks[1], (M, I)), 'uf': _xavier(ks[2], (M, M)), 'bf': jnp.zeros((M,), jnp.float32), 'wi': _xavier(ks[3], (M, I)), 'ui': _xavier(ks[4], (M, M)), 'bi': jnp.zeros((M,), jnp.float32), 'wc': _xavier(ks[5], (M, I)), 'uc': _xavier(ks[6], (M, M)), 'bc': jnp.zeros((M,), jnp.float32), 'wo': _xavier(ks[7], (O, I)), 'uo': _xavier(ks[8], (O, M)), 'bo': jnp.zeros((O,), jnp.float32), 'in_c': jnp.zeros((M,), jnp.float32)}
    _L0_ffn_in = _L0_ffn_setup()
    _d = {'L0_attn_a_x': _L0_attn_a_in['x'], 'L0_attn_a_ln1_g': _L0_attn_a_in['ln1_g'], 'L0_attn_a_ln1_b': _L0_attn_a_in['ln1_b'], 'L0_attn_a_ln2_g': _L0_attn_a_in['ln2_g'], 'L0_attn_a_ln2_b': _L0_attn_a_in['ln2_b'], 'L0_attn_a_rms_w': _L0_attn_a_in['rms_w'], 'L0_attn_a_in_proj_w': _L0_attn_a_in['in_proj_w'], 'L0_attn_a_conv_w': _L0_attn_a_in['conv_w'], 'L0_attn_a_conv_b': _L0_attn_a_in['conv_b'], 'L0_attn_a_x_proj_w': _L0_attn_a_in['x_proj_w'], 'L0_attn_a_dt_proj_w': _L0_attn_a_in['dt_proj_w'], 'L0_attn_a_dt_proj_b': _L0_attn_a_in['dt_proj_b'], 'L0_attn_a_A_log': _L0_attn_a_in['A_log'], 'L0_attn_a_D_param': _L0_attn_a_in['D_param'], 'L0_attn_a_out_proj_w': _L0_attn_a_in['out_proj_w'], 'L0_attn_a_ffn_w1': _L0_attn_a_in['ffn_w1'], 'L0_attn_a_ffn_b1': _L0_attn_a_in['ffn_b1'], 'L0_attn_a_ffn_w2': _L0_attn_a_in['ffn_w2'], 'L0_attn_a_ffn_b2': _L0_attn_a_in['ffn_b2'], 'L0_attn_b_w_att_val': _L0_attn_b_in['w_att_val'], 'L0_attn_b_wv_w': _L0_attn_b_in['wv_w'], 'L0_attn_b_wv_b': _L0_attn_b_in['wv_b'], 'L0_attn_b_out_w': _L0_attn_b_in['out_w'], 'L0_attn_b_out_b': _L0_attn_b_in['out_b'], 'L0_ffn_wf': _L0_ffn_in['wf'], 'L0_ffn_uf': _L0_ffn_in['uf'], 'L0_ffn_bf': _L0_ffn_in['bf'], 'L0_ffn_wi': _L0_ffn_in['wi'], 'L0_ffn_ui': _L0_ffn_in['ui'], 'L0_ffn_bi': _L0_ffn_in['bi'], 'L0_ffn_wc': _L0_ffn_in['wc'], 'L0_ffn_uc': _L0_ffn_in['uc'], 'L0_ffn_bc': _L0_ffn_in['bc'], 'L0_ffn_wo': _L0_ffn_in['wo'], 'L0_ffn_uo': _L0_ffn_in['uo'], 'L0_ffn_bo': _L0_ffn_in['bo'], 'L0_ffn_in_c': _L0_ffn_in['in_c']}
    _x0 = _d['L0_attn_a_x']
    _d['L0_attn_a_x'] = jax.random.normal(jax.random.fold_in(jax.random.key(seed), 1), (8, 512, 256), dtype=_x0.dtype)
    del _x0
    return _d

def reference(L0_attn_a_x, L0_attn_a_ln1_g, L0_attn_a_ln1_b, L0_attn_a_ln2_g, L0_attn_a_ln2_b, L0_attn_a_rms_w, L0_attn_a_in_proj_w, L0_attn_a_conv_w, L0_attn_a_conv_b, L0_attn_a_x_proj_w, L0_attn_a_dt_proj_w, L0_attn_a_dt_proj_b, L0_attn_a_A_log, L0_attn_a_D_param, L0_attn_a_out_proj_w, L0_attn_a_ffn_w1, L0_attn_a_ffn_b1, L0_attn_a_ffn_w2, L0_attn_a_ffn_b2, L0_attn_b_w_att_val, L0_attn_b_wv_w, L0_attn_b_wv_b, L0_attn_b_out_w, L0_attn_b_out_b, L0_ffn_wf, L0_ffn_uf, L0_ffn_bf, L0_ffn_wi, L0_ffn_ui, L0_ffn_bi, L0_ffn_wc, L0_ffn_uc, L0_ffn_bc, L0_ffn_wo, L0_ffn_uo, L0_ffn_bo, L0_ffn_in_c):

    def _L0_attn_a_ref(x, ln1_g, ln1_b, ln2_g, ln2_b, rms_w, in_proj_w, conv_w, conv_b, x_proj_w, dt_proj_w, dt_proj_b, A_log, D_param, out_proj_w, ffn_w1, ffn_b1, ffn_w2, ffn_b2):
        import jax, jax.numpy as jnp
        import numpy as np
        N_EMBED = 256
        D_STATE = 16
        D_CONV = 4
        DT_RANK = 64
        BATCH, SEQ = (4, 512)

        def layernorm(x, g, b, eps=1e-05):
            mu = jnp.mean(x, -1, keepdims=True)
            var = jnp.mean((x - mu) ** 2, -1, keepdims=True)
            return (x - mu) * jax.lax.rsqrt(var + eps) * g + b

        def rmsnorm(x, w, eps=1e-05):
            return x * jax.lax.rsqrt(jnp.mean(x * x, -1, keepdims=True) + eps) * w

        def mamba_mixer(x, in_proj_w, conv_w, conv_b, x_proj_w, dt_proj_w, dt_proj_b, A_log, D_param, out_proj_w):
            Bt, L, D = x.shape
            ED = in_proj_w.shape[1] // 2
            N = A_log.shape[1]
            K = conv_w.shape[-1]
            xz = x @ in_proj_w
            xi, z = jnp.split(xz, 2, axis=-1)
            xc = jnp.swapaxes(xi, 1, 2)
            xc = jax.lax.conv_general_dilated(xc, conv_w[:, None, :], window_strides=(1,), padding=[(K - 1, 0)], feature_group_count=ED, dimension_numbers=('NCH', 'OIH', 'NCH'))
            xc = jnp.swapaxes(xc + conv_b[None, :, None], 1, 2)
            xc = jax.nn.silu(xc)
            dbc = xc @ x_proj_w
            dt_rank = dt_proj_w.shape[0]
            delta = jax.nn.softplus(dbc[..., :dt_rank] @ dt_proj_w + dt_proj_b)
            Bm = dbc[..., dt_rank:dt_rank + N]
            Cm = dbc[..., dt_rank + N:]
            A = -jnp.exp(A_log)
            deltaA = jnp.exp(delta[..., None] * A)
            BX = (delta * xc)[..., None] * Bm[:, :, None, :]

            def step(h, inp):
                dA, bx, c = inp
                h = dA * h + bx
                return (h, jnp.einsum('ben,bn->be', h, c))
            h0 = jnp.zeros((Bt, ED, N), x.dtype)
            _, ys = jax.lax.scan(step, h0, (jnp.swapaxes(deltaA, 0, 1), jnp.swapaxes(BX, 0, 1), jnp.swapaxes(Cm, 0, 1)))
            y = jnp.swapaxes(ys, 0, 1) + D_param * xc
            y = y * jax.nn.silu(z)
            return y @ out_proj_w
        h = layernorm(x, ln1_g, ln1_b)
        h = h + mamba_mixer(rmsnorm(h, rms_w), in_proj_w, conv_w, conv_b, x_proj_w, dt_proj_w, dt_proj_b, A_log, D_param, out_proj_w)
        x = x + h
        h2 = layernorm(x, ln2_g, ln2_b)
        x = x + (jax.nn.relu(h2 @ ffn_w1 + ffn_b1) @ ffn_w2 + ffn_b2)
        return x

    def _L0_attn_b_ref(x, w_att_val, wv_w, wv_b, out_w, out_b):
        import jax, jax.numpy as jnp
        import numpy as np
        B, T, E, H = (2, 512, 256, 16)
        D = E // H
        b, t, e = x.shape
        h, d, _ = w_att_val.shape
        x_h = x.reshape(b, t, h, d).transpose(0, 2, 1, 3)
        xw = jnp.einsum('bhtd,hde->bhte', x_h, w_att_val)
        att = jnp.einsum('bhte,bhse->bhts', xw, x_h) / jnp.sqrt(jnp.asarray(d, x.dtype))
        att = jax.nn.softmax(att, axis=-1)
        vx = x @ wv_w.T + wv_b
        vx = vx.reshape(b, t, h, d).transpose(0, 2, 1, 3)
        o = jnp.einsum('bhts,bhsd->bhtd', att, vx)
        o = o.transpose(0, 2, 1, 3).reshape(b, t, e)
        return o @ out_w.T + out_b

    def _L0_ffn_ref(x, wf, uf, bf, wi, ui, bi, wc, uc, bc, wo, uo, bo, in_c):
        import jax, jax.numpy as jnp
        import numpy as np
        from jax import lax
        T, B, I, M, O = (64, 64, 256, 256, 256)

        def _xavier(key, shape):
            fan_out, fan_in = shape
            limit = float(np.sqrt(6.0 / (fan_in + fan_out)))
            return jax.random.uniform(key, shape, jnp.float32, -limit, limit)
        batch = x.shape[1]
        c0 = jnp.broadcast_to(in_c, (batch, in_c.shape[0]))

        def step(c, xt):
            ft = jax.nn.sigmoid(xt @ wf.T + c @ uf.T + bf)
            it = jax.nn.sigmoid(xt @ wi.T + c @ ui.T + bi)
            gt = jnp.tanh(xt @ wc.T + c @ uc.T + bc)
            c = ft * c + it * gt
            return (c, None)
        c_final, _ = lax.scan(step, c0, x)
        h = jnp.tanh(jnp.einsum('tbi,oi->tbo', x, wo) + c_final @ uo.T + bo)
        return h
    x = L0_attn_a_x
    x = x + _L0_attn_a_ref(_layernorm(x, axis=-1), L0_attn_a_ln1_g, L0_attn_a_ln1_b, L0_attn_a_ln2_g, L0_attn_a_ln2_b, L0_attn_a_rms_w, L0_attn_a_in_proj_w, L0_attn_a_conv_w, L0_attn_a_conv_b, L0_attn_a_x_proj_w, L0_attn_a_dt_proj_w, L0_attn_a_dt_proj_b, L0_attn_a_A_log, L0_attn_a_D_param, L0_attn_a_out_proj_w, L0_attn_a_ffn_w1, L0_attn_a_ffn_b1, L0_attn_a_ffn_w2, L0_attn_a_ffn_b2)
    x = x + _L0_ffn_ref(_layernorm(x, axis=-1), L0_ffn_wf, L0_ffn_uf, L0_ffn_bf, L0_ffn_wi, L0_ffn_ui, L0_ffn_bi, L0_ffn_wc, L0_ffn_uc, L0_ffn_bc, L0_ffn_wo, L0_ffn_uo, L0_ffn_bo, L0_ffn_in_c)
    x = x + _L0_attn_b_ref(_layernorm(x, axis=-1), L0_attn_b_w_att_val, L0_attn_b_wv_w, L0_attn_b_wv_b, L0_attn_b_out_w, L0_attn_b_out_b)
    x = x + _L0_ffn_ref(_layernorm(x, axis=-1), L0_ffn_wf, L0_ffn_uf, L0_ffn_bf, L0_ffn_wi, L0_ffn_ui, L0_ffn_bi, L0_ffn_wc, L0_ffn_uc, L0_ffn_bc, L0_ffn_wo, L0_ffn_uo, L0_ffn_bo, L0_ffn_in_c)
    return x

_drawn_inputs = setup_inputs


def setup_inputs(seed=0):
    import zlib

    import numpy as np

    out = dict(_drawn_inputs(seed))
    spreads = {'L0_attn_a_ln1_g': (1.0, 0.2),
     'L0_attn_a_ln1_b': (0.0, 0.1),
     'L0_attn_a_ln2_g': (1.0, 0.2),
     'L0_attn_a_ln2_b': (0.0, 0.1),
     'L0_attn_a_rms_w': (1.0, 0.2),
     'L0_attn_a_conv_b': (0.0, 0.1),
     'L0_attn_a_dt_proj_b': (-4.600166320800781, 0.2),
     'L0_attn_a_D_param': (1.0, 0.2),
     'L0_attn_a_ffn_b1': (0.0, 0.1),
     'L0_attn_a_ffn_b2': (0.0, 0.1),
     'L0_attn_b_wv_b': (0.0, 0.1),
     'L0_attn_b_out_b': (0.0, 0.1),
     'L0_ffn_bf': (0.0, 0.1),
     'L0_ffn_bi': (0.0, 0.1),
     'L0_ffn_bc': (0.0, 0.1),
     'L0_ffn_bo': (0.0, 0.1),
     'L0_ffn_in_c': (0.0, 0.1)}
    factors = {}
    for name, (base, spread) in spreads.items():
        noise = np.random.default_rng([zlib.crc32(name.encode()), seed]).standard_normal(out[name].shape)
        drawn = base * np.exp(spread * noise) if base else spread * noise
        out[name] = jnp.asarray(drawn.astype(out[name].dtype))
    for name, factor in factors.items():
        out[name] = (out[name] * factor).astype(out[name].dtype)
    return out
```

```python
import numpy as np
import concourse.bass as bass
from concourse import mybir
from contextlib import ExitStack

F32 = mybir.dt.float32
BF16 = mybir.dt.bfloat16
ALU = mybir.AluOpType
ACT = mybir.ActivationFunctionType
AXIS = mybir.AxisListType

P = 128
D = 256
NB, L = 8, 512
NT = L // P
NF = D // P
NS = 16
SG = 4
EB = P // SG
NJ = D // EB
TAPS = 4
RANK = 64
HID = 4 * D
NH, HD = 16, 16
HU = NH // 2
VW = 32
EPS = 1e-5

VEC = {}
for _n, _w in [("ln2_g", 2), ("ln2_b", 2), ("rms_w", 2), ("conv_w", 8), ("conv_b", 2), ("dt_b", 2),
               ("D", 2), ("ffn_b1", 8), ("bf", 2), ("bi", 2), ("bc", 2), ("in_c", 2), ("A_log", 32)]:
    VEC[_n] = (sum(w for _, w in VEC.values()), _w)
NVEC = sum(w for _, w in VEC.values())
ROWS = ["ln1_g", "ln1_b", "ffn_b2", "bo", "wv_b", "out_b"]


OPS = {
    "activation": lambda e: e.activation, "bn_stats": lambda e: e.bn_stats, "bn_aggr": lambda e: e.bn_aggr,
    "dma_start": lambda e: e.dma_start, "matmul": lambda e: e.matmul, "memset": lambda e: e.memset,
    "reciprocal": lambda e: e.reciprocal, "scalar_tensor_tensor": lambda e: e.scalar_tensor_tensor,
    "tensor_copy": lambda e: e.tensor_copy, "tensor_reduce": lambda e: e.tensor_reduce,
    "tensor_scalar": lambda e: e.tensor_scalar, "tensor_tensor": lambda e: e.tensor_tensor,
    "tensor_tensor_reduce": lambda e: e.tensor_tensor_reduce, "tensor_tensor_scan": lambda e: e.tensor_tensor_scan,
    "transpose": lambda e: e.transpose,
}


def op(name, *operands, **modes):
    return name, operands, modes


class Queue:

    def __init__(self, sem):
        self.sem, self.count, self.passed, self.steps = sem, 0, {}, []

    def waits(self, after):
        need = {}
        for mark in after:
            if mark is None:
                continue
            if isinstance(mark, list):
                inner = self.waits(mark)
                for s, v in inner:
                    need[s] = max(need.get(s, 0), v)
                continue
            s, v = mark
            if v > self.passed.get(s, 0):
                need[s] = max(need.get(s, 0), v)
        return list(need.items())

    def put(self, issue, after, sem, by):
        need = self.waits(after)
        for s, v in need:
            self.passed[s] = v
        self.steps.append((need, issue, sem, by))

    def do(self, issue, *after):
        self.count += 1
        self.put(issue, after, self.sem, 1)
        return (self.sem, self.count)

    def quiet(self, issue, *after):
        self.put(issue, after, None, 0)

    def emit(self, eng):
        for need, issue, sem, by in self.steps:
            for s, v in need:
                eng.wait_ge(s, v)
            name, operands, modes = issue
            ins = OPS[name](eng)(*operands, **modes)
            if sem is not None:
                ins.then_inc(sem, by)


class Arrival:

    def __init__(self, sem):
        self.sem, self.count = sem, 0

    def load(self, queue, out, in_, *after):
        self.count += 16
        queue.put(op("dma_start", out, in_), after, self.sem, 16)
        return (self.sem, self.count)


class Ring:

    def __init__(self, items):
        self.items = [(x, None) for x in items]

    def take(self):
        return self.items.pop(0)

    def give(self, item, *marks):
        self.items.append((item, list(marks)))


def grab(ring):
    while not ring.items:
        yield
    return ring.take()


def weave(*streams):
    live = [[g, 0, n] for g, n in streams]
    while live:
        s = min(live, key=lambda x: x[1] / x[2])
        try:
            next(s[0])
            s[1] += 1
        except StopIteration:
            live.remove(s)


def build(nc, t_in, out):
    ctx = ExitStack()
    with ctx:
        sem = lambda name: ctx.enter_context(nc.semaphore(name))
        pe, act, dve, pool, sp = (Queue(sem(n)) for n in
                                  ("pe_done", "act_done", "dve_done", "pool_done", "sp_done"))
        arrive = lambda name: Arrival(sem(name))

        ARENA = 52900
        arena = ctx.enter_context(nc.sbuf_tensor("arena", [P, ARENA], F32))
        top = [0]

        def sb(*shape, dt=F32):
            n = int(np.prod(shape))
            words = n if dt is F32 else (n + 1) // 2
            at = top[0]
            top[0] += words
            assert top[0] <= ARENA, (top[0], ARENA)
            v = arena[:, at:at + words]
            if dt is not F32:
                v = v.bitcast(dt)
            if len(shape) > 1:
                names = " ".join(f"d{i}" for i in range(len(shape)))
                v = v.rearrange(f"p ({names}) -> p {names}",
                                **{f"d{i}": s for i, s in enumerate(shape)})
            return v

        psum = ctx.enter_context(nc.psum_tensor("psum", [P, 8, L], F32))
        bank = lambda i: psum[:, i, :]
        pair = lambda i: psum[:, 2 * i:2 * i + 2, :]

        dram = lambda name, shape, dt: nc.dram_tensor(name, shape, dt, kind="Internal").ap()
        dd_dram = [dram(f"dd{i}", (D, 2, L), F32) for i in range(2)]
        bc_dram = [dram(f"bc{i}", (2 * NS, L), F32) for i in range(2)]
        part_dram = [dram(f"parts{i}", (2, 3, D, L), BF16) for i in range(2)]
        max_dram = [dram(f"max{i}", (3, HU * NT, P), BF16) for i in range(2)]
        x_dram = [dram(f"x_after_{n}", (NB, NT, P, D), F32) for n in ("mamba", "attention")]
        xwo_dram = [dram(f"xwo_{n}", (NB, NT, P, D), F32) for n in ("first", "second")]

        ident = sb(P)
        sel = sb(EB)
        vec = sb(NVEC)
        rows = sb(len(ROWS), D)
        wx = sb(NF, 3 * D)
        uh = sb(NF, 3 * D)
        wo = sb(NF, D)
        uo = sb(NF, D)
        half_bias = sb(4)
        conv_half = sb(10)
        A_neg = sb(NJ * SG)
        c_state = sb(NF, L)
        stats = [sb(NT, 6) for _ in range(2)]
        mv = [sb(NT, 2) for _ in range(2)]
        rstd = [sb(NT) for _ in range(2)]
        neg_half = sb(NT)
        col = lambda name, i=0: vec[:, VEC[name][0] + i:VEC[name][0] + i + 1]
        row = lambda name: rows[:, ROWS.index(name), :]
        over_tiles = lambda r: r.unsqueeze(1).to_broadcast([P, NT, D])
        shared_top = top[0]

        w_small, w_mamba, w_ffn, w_gate, w_att = (arrive(f"weights_{n}") for n in
                                                  ("small", "mamba", "ffn", "gate", "attention"))
        x_in = [arrive(f"x_in{i}") for i in range(2)]
        kn = lambda ap: ap.rearrange("(k p) n -> p k n", p=P)

        w_in = sb(NF, 2 * D)
        w_xp = sb(NF, RANK + 2 * NS)
        w_dt = sb(D)
        w_out = sb(NF, D)
        w1 = sb(NF, HID)
        w2 = sb(HID // P, D)
        xb = [sb(NT, D) for _ in range(2)]
        xh = [sb(NT, D) for _ in range(2)]
        xi_pad = sb(NF, TAPS - 1 + L)
        xc = [sb(NF, L) for _ in range(2)]
        sz = [sb(NF, L) for _ in range(2)]
        dbc = sb(L)
        dd_out = sb(NF, 2, L)
        ddb = sb(NJ, 2, L)
        bcb = [sb(2, 2, L) for _ in range(2)]
        dA_ring = Ring([sb(2, L) for _ in range(3)])
        hb_ring = Ring([sb(2, L) for _ in range(6)])
        tmp = Ring([sb(NT * D) for _ in range(6)])
        tok = lambda v: v.rearrange("p (t d) -> p t d", t=NT)
        feat = lambda v: v.rearrange("p (f t) -> p f t", f=NF)

        load = w_small.load
        load(sp, vec, t_in["vec"])
        load(sp, ident, t_in["ident"])
        x_loads = {}

        def load_x(b, *after):
            x_loads[b] = x_in[b % 2].load(sp, xb[b % 2], t_in["x"][b].rearrange("(t p) d -> p t d", p=P), *after)
        load_x(0)
        load(sp, sel, t_in["sel"])
        small_ready = load(sp, rows, t_in["rows"].partition_broadcast(P))
        w_mamba.load(sp, w_in, kn(t_in["w_in"]))
        w_mamba.load(sp, w_xp, kn(t_in["w_xp"]))
        w_mamba.load(sp, w_dt[0:RANK, :], t_in["w_dt"])
        mamba_ready = w_mamba.load(sp, w_out, kn(t_in["w_out"]))
        w_ffn.load(sp, w1, kn(t_in["w1"]))
        ffn_ready = w_ffn.load(sp, w2, kn(t_in["w2"]))
        w_gate.load(sp, wx, kn(t_in["wx"]))
        w_gate.load(sp, uh, kn(t_in["uh"]))
        w_gate.load(sp, wo, kn(t_in["wo"]))
        gate_ready = w_gate.load(sp, uo, kn(t_in["uo"]))

        c0 = VEC["bf"][0]
        made_bias = dve.do(op("tensor_scalar", half_bias, vec[:, c0:c0 + 4], 0.5, None, ALU.mult), small_ready)
        c1 = VEC["conv_w"][0]
        made_conv = dve.do(op("tensor_scalar", conv_half, vec[:, c1:c1 + 10], 0.5, None, ALU.mult))
        c2 = VEC["A_log"][0]
        exp_A = act.do(op("activation", A_neg, vec[:, c2:c2 + NJ * SG], ACT.Exp), small_ready)
        made_A = dve.do(op("tensor_scalar", A_neg, A_neg, -1.0, None, ALU.mult), exp_A)
        minus_half = pool.do(op("memset", neg_half, -0.5))
        zero_pad = pool.do(op("memset", xi_pad[:, :, 0:TAPS - 1], 0.0))

        def start_state(*after):
            z = dve.do(op("memset", c_state, 0.0), *after)
            for f in range(NF):
                z0 = z
                z = dve.do(op("tensor_scalar", c_state[:, f, :], c_state[:, f, :], col("in_c", f), None, ALU.add), z0, small_ready)
            return z

        def normalise(src, dst, ready, which, free=None):
            st, m, r = stats[which], mv[which], rstd[which]
            for t in range(NT):
                a = dve.do(op("bn_stats", st[:, t, :], src[:, t, :]), ready)
            for t in range(NT):
                b_ = dve.do(op("bn_aggr", m[:, t, :], st[:, t, :]), a)
            c = dve.do(op("tensor_scalar", r.unsqueeze(2), m[:, :, 1:2], EPS, None, ALU.add), b_)
            c = pool.do(op("tensor_tensor", r, r, neg_half, ALU.pow), c, minus_half)
            for t in range(NT):
                d_ = dve.do(op("tensor_scalar", dst[:, t, :], src[:, t, :], m[:, t, 0:1], r[:, t:t + 1],
                                                           ALU.subtract, ALU.mult), c, free)
            return d_

        def turn(src, ready, to, free):
            for f in range(NF):
                for t in range(NT):
                    ps = to[:, f, t * P:(t + 1) * P]
                    issue = op("transpose", ps, src[:, t, f * P:(f + 1) * P], ident)
                    if f == NF - 1 and t == NT - 1:
                        done = pe.do(issue, ready, free, small_ready)
                    else:
                        pe.quiet(issue, ready, free, small_ready)
            return done

        def product(outs, *after):
            n = sum(len(terms) for _, terms in outs)
            i = 0
            for o, terms in outs:
                for k, (l, r) in enumerate(terms):
                    i += 1
                    issue = op("matmul", o, l, r, start=k == 0, stop=k == len(terms) - 1)
                    if i == n:
                        return pe.do(issue, *after)
                    pe.quiet(issue, *after)

        def halves(v):
            return v.rearrange("p b (u d) -> p (b u) d", u=NT // 2)

        def gate_step(b, x_new, ready, x_give, banks, tmp, state, xwo_arrive, xwo_out):
            xr, free = yield from grab(tmp)
            xr_done = normalise(x_new, tok(xr), ready, 1, free)
            x_give(xr_done)
            yield
            xrT, free = yield from grab(tmp)
            ps, ps_free = yield from grab(banks)
            turned = turn(tok(xr), xr_done, ps, ps_free)
            tmp.give(xr, turned)
            yield
            xrT_done = act.do(op("activation", feat(xrT), ps, ACT.Copy), turned, free)
            banks.give(ps, xrT_done)
            yield
            ps, ps_free = yield from grab(banks)
            hv = halves(ps)
            wo_done = product([(hv[:, t, :], [(feat(xrT)[:, k, t * P:(t + 1) * P], wo[:, k, :]) for k in range(NF)])
                               for t in range(NT)], xrT_done, ps_free, gate_ready)
            xwo, free = yield from grab(tmp)
            xwo_done = dve.do(op("tensor_tensor", tok(xwo), hv, over_tiles(row("bo")), ALU.add), wo_done, free)
            banks.give(ps, xwo_done)
            xwo_sent = xwo_arrive[b % 2].load(sp, xwo_out[b].rearrange("t p d -> p t d"), tok(xwo), xwo_done)
            tmp.give(xwo, xwo_sent)
            state["sent"].append(xwo_sent)
            yield
            gates = []
            for g, (fn, sc) in enumerate([(ACT.Tanh, 0.5), (ACT.Tanh, 0.5), (ACT.Tanh, 1.0)]):
                ps, ps_free = yield from grab(banks)
                for f in range(NF):
                    w = slice(g * D + f * P, g * D + (f + 1) * P)
                    mm = product([(ps[:, f, :], [(wx[:, k, w], feat(xrT)[:, k, :]) for k in range(NF)]
                                   + [(uh[:, k, w], c_state[:, k, :]) for k in range(NF)])],
                                 xrT_done, ps_free, gate_ready, state["c"])
                    yield
                gt, free = yield from grab(tmp)
                for f in range(NF):
                    bias = half_bias[:, 2 * g + f:2 * g + f + 1] if g < 2 else col("bc", f)
                    done = act.do(op("activation", feat(gt)[:, f, :], ps[:, f, :], fn, bias=bias, scale=sc), mm, free, made_bias)
                banks.give(ps, done)
                gates.append((gt, done))
                yield
            tmp.give(xrT, mm)
            (gf, f_ok), (gi, i_ok), (gc, c_ok) = gates
            a = dve.do(op("scalar_tensor_tensor", feat(gf), feat(gf), 1.0, c_state, ALU.add, ALU.mult), f_ok, state["c"])
            d_ = dve.do(op("scalar_tensor_tensor", feat(gi), feat(gi), 1.0, feat(gc), ALU.add, ALU.mult), i_ok, c_ok)
            s = dve.do(op("tensor_tensor", gf, gf, gi, ALU.add), a, d_)
            state["c"] = dve.do(op("tensor_scalar", c_state, feat(gf), 0.5, None, ALU.mult), s, mm)
            for gt in (gf, gi, gc):
                tmp.give(gt, state["c"])
            yield

        cleared = [dve.do(op("memset", pair(i), 0.0)) for i in range(3)]
        banks1 = Ring([pair(0), pair(1), pair(2)])
        banks1.items = [(x, [m]) for (x, _), m in zip(banks1.items, cleared)]
        y_pair = pair(3)
        state = {"c": start_state(), "sent": []}
        bc_sent, bc_in = [arrive(f"bc_out{i}") for i in range(2)], [arrive(f"bc_in{i}") for i in range(2)]
        dd_sent, dd_in = arrive("dd_out"), [arrive(f"dd_in{i}") for i in range(NJ)]
        x_sent = [arrive(f"x_sent{i}") for i in range(2)]
        xwo_sent = [arrive(f"xwo_sent{i}") for i in range(2)]
        S = {"xc": {}, "sz": {}, "xh": {}, "xb2": {}, "dd": {}, "bc": {}, "y_free": None, "yT": {}, "dd_read": {},
             "bc_read": {}, "xi_free": None, "dbc_free": None, "dd_out_free": None, "xc_free": [None, None],
             "sz_free": [None, None], "xh_free": [None, None], "ddb_free": [None] * NJ, "bcb_free": [None, None],
             "x_sent": {}, "bc_src": {}, "dd_src": {}, "bcb_freed": [-1, -1],
             "ddb_freed": [-1] * NJ}

        def mamba_front(b):
            i = b % 2
            x_ok = x_loads[b]
            xn, f1 = yield from grab(tmp)
            xn_ok = normalise(xb[i], tok(xn), x_ok, 0, f1)
            S["xb2"][b] = pool.do(op("tensor_tensor", xb[i], xb[i], over_tiles(row("ffn_b2")), ALU.add), xn_ok, small_ready)
            yield
            h, f2 = yield from grab(tmp)
            h0_ok = normalise(tok(xn), tok(h), xn_ok, 0, f2)
            yield
            hg_ok = pool.do(op("tensor_tensor", tok(h), tok(h), over_tiles(row("ln1_g")), ALU.mult), h0_ok, small_ready)
            h_ok = pool.do(op("tensor_tensor", tok(h), tok(h), over_tiles(row("ln1_b")), ALU.add), hg_ok)
            S["xh"][b] = pool.do(op("tensor_tensor", xh[i], tok(xn), tok(h), ALU.add), h_ok, S["xh_free"][i])
            yield
            yield
            m, f3 = yield from grab(tmp)
            for t in range(NT):
                q = dve.do(op("tensor_tensor_reduce", out=tok(m)[:, t, :], in0=tok(h)[:, t, :], in1=tok(h)[:, t, :],
                                                                 scale=1.0, scalar=0.0, op0=ALU.mult, op1=ALU.add,
                                                                 accum_out=rstd[0][:, t:t + 1]), h_ok, f3)
            q = dve.do(op("tensor_scalar", rstd[0], rstd[0], 1.0 / D, EPS, ALU.mult, ALU.add), q)
            q = pool.do(op("tensor_tensor", rstd[0], rstd[0], neg_half, ALU.pow), q)
            for t in range(NT):
                m_ok = dve.do(op("tensor_scalar", tok(m)[:, t, :], tok(h)[:, t, :], rstd[0][:, t:t + 1], None, ALU.mult), q)
            tmp.give(xn, S["xh"][b])
            tmp.give(h, m_ok, S["xh"][b])
            yield
            ps, pf = yield from grab(banks1)
            turned = turn(tok(m), m_ok, ps, pf)
            tmp.give(m, turned)
            mT, f4 = yield from grab(tmp)
            yield
            for f in range(NF):
                mT_ok = act.do(op("activation", feat(mT)[:, f, :], ps[:, f, :], ACT.Copy, scale=col("rms_w", f)), turned, f4)
            banks1.give(ps, mT_ok)
            yield
            mms = []
            for part in range(2):
                ps, pf = yield from grab(banks1)
                mm = product([(ps[:, f, :], [(w_in[:, k, part * D + f * P:part * D + (f + 1) * P], feat(mT)[:, k, :])
                                             for k in range(NF)]) for f in range(NF)], mT_ok, pf, mamba_ready)
                mms.append((ps, mm))
                yield
            tmp.give(mT, mms[1][1])
            ps, mm = mms[0]
            xi_ok = act.do(op("activation", xi_pad[:, :, TAPS - 1:], mms[0][0], ACT.Copy), mm, S["xi_free"], zero_pad)
            banks1.give(ps, xi_ok)
            ps, mm = mms[1]
            z_ok = act.do(op("activation", sz[i], mms[1][0], ACT.Copy, scale=0.5), mm, S["sz_free"][i])
            banks1.give(ps, z_ok)
            yield
            cv, fc = yield from grab(tmp)
            for f in range(NF):
                w = lambda k, f=f: conv_half[:, f * TAPS + k:f * TAPS + k + 1]
                c_ok = dve.do(op("tensor_scalar", feat(cv)[:, f, :], xi_pad[:, f, TAPS - 1:], w(TAPS - 1),
                                                                  conv_half[:, 8 + f:9 + f], ALU.mult, ALU.add), xi_ok, fc, made_conv)
                for k in range(TAPS - 1):
                    c_ok = dve.do(op("scalar_tensor_tensor", feat(cv)[:, f, :], xi_pad[:, f, k:k + L], w(k),
                                                                                  feat(cv)[:, f, :], ALU.mult, ALU.add), c_ok)
                yield
            S["xi_free"] = c_ok
            th, ft = yield from grab(tmp)
            tz, fz = yield from grab(tmp)
            th_ok = act.do(op("activation", th, cv, ACT.Tanh), c_ok, ft)
            tz_ok = act.do(op("activation", feat(tz), sz[i], ACT.Tanh), z_ok, fz)
            yield
            xc_ok = dve.do(op("scalar_tensor_tensor", xc[i], feat(th), 1.0, feat(cv), ALU.add, ALU.mult), th_ok, S["xc_free"][i])
            S["sz"][b] = dve.do(op("scalar_tensor_tensor", sz[i], feat(tz), 1.0, sz[i], ALU.add, ALU.mult), tz_ok)
            S["xc"][b] = xc_ok
            for v in (cv, th, tz):
                tmp.give(v, S["sz"][b])
            yield
            ps, pf = yield from grab(banks1)
            nr = RANK + 2 * NS
            mm = product([(ps[0:nr, 0, :], [(w_xp[:, k, :], xc[i][:, k, :]) for k in range(NF)])], xc_ok, pf)
            dbc_ok = act.do(op("activation", dbc[0:nr, :], ps[0:nr, 0, :], ACT.Copy), mm, S["dbc_free"])
            banks1.give(ps, dbc_ok)
            yield
            sent = bc_sent[i].load(sp, bc_dram[i], dbc[RANK:nr, :], dbc_ok, S["bc_read"].get(b - 2))
            src = bc_dram[i].rearrange("(c s q g) t -> s q c g t", c=2, s=SG, q=2)
            ps, pf = yield from grab(banks1)
            mm = product([(ps[:, f, :], [(w_dt[0:RANK, f * P:(f + 1) * P], dbc[0:RANK, :])]) for f in range(NF)], dbc_ok, pf)
            S["dbc_free"] = [mm, sent]
            S["bc_src"][b] = (src, sent)
            spread()
            v, fv = yield from grab(tmp)
            for f in range(NF):
                v_ok = act.do(op("activation", feat(v)[:, f, :], ps[:, f, :], ACT.Identity, bias=col("dt_b", f)), mm, fv)
            banks1.give(ps, v_ok)
            yield
            u, fu = yield from grab(tmp)
            a_ok = dve.do(op("scalar_tensor_tensor", u, v, -1.0, v, ALU.mult, ALU.min), v_ok, fu)
            u_ok = act.do(op("activation", u, u, ACT.Exp), a_ok)
            yield
            ln, fl = yield from grab(tmp)
            ln_ok = act.do(op("activation", ln, u, ACT.Ln, bias=1.0), u_ok, fl)
            w_, fw = yield from grab(tmp)
            w_ok = dve.do(op("tensor_scalar", w_, u, 1.0, -1.0, ALU.add, ALU.add), u_ok, fw)
            r_ok = dve.do(op("tensor_tensor", w_, u, w_, ALU.subtract), w_ok)
            s_ok = dve.do(op("tensor_tensor", ln, ln, w_, ALU.add), r_ok, ln_ok)
            d_ok = dve.do(op("scalar_tensor_tensor", dd_out[:, :, 0, :], feat(v), 0.0, feat(ln), ALU.max, ALU.add), s_ok,
                          S["dd_out_free"])
            tmp.give(u, r_ok, ln_ok)
            for z in (ln, w_, v):
                tmp.give(z, d_ok)
            yield
            du_ok = pool.do(op("tensor_tensor", dd_out[:, :, 1, :], dd_out[:, :, 0, :], xc[i], ALU.mult), d_ok, xc_ok)
            yield
            sent = dd_sent.load(sp, dd_dram[i].rearrange("(f p) c t -> p f c t", p=P), dd_out, d_ok, du_ok, S["dd_read"].get(b - 2))
            S["dd_out_free"] = sent
            yield
            S["dd_src"][b] = sent
            spread()
            yield

        def spread():
            for b in range(NB):
                for q in range(2):
                    if b in S["bc_src"] and (b, q) not in S["bc"] and S["bcb_freed"][q] == b - 1:
                        src, sent = S["bc_src"][b]
                        for s in range(SG):
                            got = bc_in[q].load(sp, bcb[q][s * EB:(s + 1) * EB], src[s, q].partition_broadcast(EB), sent,
                                                S["bcb_free"][q])
                        S["bc"][b, q] = got
                        S["bc_read"].setdefault(b, []).append(got)
                for j in range(NJ):
                    if b in S["dd_src"] and (b, j) not in S["dd"] and S["ddb_freed"][j] == b - 1:
                        for s in range(SG):
                            got = dd_in[j].load(sp, ddb[s * EB:(s + 1) * EB, j, :, :], dd_dram[b % 2][j * EB:(j + 1) * EB],
                                                S["dd_src"][b], S["ddb_free"][j])
                        S["dd"][b, j] = got
                        S["dd_read"].setdefault(b, []).append(got)

        def mamba_scan(b):
            for q in range(2):
                for f in range(NF):
                    held = []
                    for jj in range(NJ // NF):
                        j = f * (NJ // NF) + jj
                        dA, fa = dA_ring.take()
                        hb, fh = hb_ring.take()
                        for g in range(2):
                            ai = j * SG + 2 * q + g
                            dA_ok = act.do(op("activation", dA[:, g, :], ddb[:, j, 0, :], ACT.Exp,
                                           scale=A_neg[:, ai:ai + 1]), S["dd"][b, j], fa, made_A)
                        bx_ok = pool.do(op("tensor_tensor", hb, ddb[:, j, 1:2, :].to_broadcast([P, 2, L]),
                                        bcb[q][:, 0, :, :], ALU.mult), S["dd"][b, j], S["bc"][b, q], fh)
                        for g in range(2):
                            h_ok = dve.do(op("tensor_tensor_scan", hb[:, g, :], dA[:, g, :], hb[:, g, :], 0.0,
                                          ALU.mult, ALU.add), dA_ok, bx_ok)
                        dA_ring.give(dA, h_ok)
                        hc_ok = dve.do(op("tensor_tensor", hb, hb, bcb[q][:, 1, :, :], ALU.mult), h_ok)
                        if q == 1:
                            S["ddb_free"][j], S["ddb_freed"][j] = [dA_ok, bx_ok], b
                            spread()
                        held.append((hb, hc_ok))
                        yield
                    for g in range(2):
                        for jj, (hb, hc_ok) in enumerate(held):
                            issue = op("matmul", 
                                y_pair[jj * EB:(jj + 1) * EB, f, :], sel, hb[:, g, :], start=(q == 0 and g == 0), stop=(q == 1 and g == 1))
                            if g == 1 and jj == len(held) - 1:
                                y_ok = pe.do(issue, hc_ok)
                            else:
                                pe.quiet(issue, hc_ok, S["y_free"], small_ready)
                    for hb, _ in held:
                        hb_ring.give(hb, y_ok)
                    if q == 1:
                        i = b % 2
                        a = dve.do(op("scalar_tensor_tensor", xc[i][:, f, :], xc[i][:, f, :], col("D", f), y_pair[:, f, :],
                                   ALU.mult, ALU.add), y_ok, S["dd_out_free"])
                        S["yT"][b] = dve.do(op("tensor_tensor", xc[i][:, f, :], xc[i][:, f, :], sz[i][:, f, :], ALU.mult), a)
                        if f == NF - 1:
                            S["y_free"] = a
                            S["sz_free"][i] = S["yT"][b]
                    yield
                S["bcb_free"][q], S["bcb_freed"][q] = hc_ok, b
                spread()

        def mamba_back(b):
            i = b % 2
            ps, pf = yield from grab(banks1)
            hv = halves(ps)
            mm = product([(hv[:, t, :], [(xc[i][:, k, t * P:(t + 1) * P], w_out[:, k, :]) for k in range(NF)]) for t in range(NT)],
                         S["yT"][b], pf)
            S["xc_free"][i] = mm
            yield
            x1, f1 = yield from grab(tmp)
            x1_ok = dve.do(op("tensor_tensor", tok(x1), hv, xh[i], ALU.add), mm, f1, S["xh"][b])
            banks1.give(ps, x1_ok)
            S["xh_free"][i] = x1_ok
            h2, f2 = yield from grab(tmp)
            h2_ok = normalise(tok(x1), tok(h2), x1_ok, 1, f2)
            s_ok = pool.do(op("tensor_tensor", xb[i], xb[i], tok(x1), ALU.add), x1_ok, S["xb2"][b])
            tmp.give(x1, s_ok, h2_ok)
            yield
            ps, pf = yield from grab(banks1)
            turned = turn(tok(h2), h2_ok, ps, pf)
            tmp.give(h2, turned)
            hT, f3 = yield from grab(tmp)
            yield
            for f in range(NF):
                hT_ok = act.do(op("activation", feat(hT)[:, f, :], ps[:, f, :], ACT.Identity, scale=col("ln2_g", f),
                                                                  bias=col("ln2_b", f)), turned, f3)
            banks1.give(ps, hT_ok)
            yield
            acc, acc_free = yield from grab(banks1)
            hv2 = halves(acc)
            nch = HID // P // 2
            for c in range(nch):
                ps, pf = yield from grab(banks1)
                mm = product([(ps[:, u, :], [(w1[:, k, (2 * c + u) * P:(2 * c + u + 1) * P], feat(hT)[:, k, :]) for k in range(NF)])
                              for u in range(2)], hT_ok, pf, ffn_ready)
                r, fr = yield from grab(tmp)
                yield
                for u in range(2):
                    r_ok = act.do(op("activation", feat(r)[:, u, :], ps[:, u, :], ACT.Relu,
                                  bias=col("ffn_b1", 2 * c + u)), mm, fr)
                banks1.give(ps, r_ok)
                yield
                for t in range(NT):
                    for u in range(2):
                        issue = op("matmul", hv2[:, t, :], feat(r)[:, u, t * P:(t + 1) * P], w2[:, 2 * c + u, :],
                                start=(c == 0 and u == 0 and t % 2 == 0), stop=(c == nch - 1 and u == 1), skip_group_check=True)
                        if t == NT - 1 and u == 1:
                            mm2 = pe.do(issue, r_ok)
                        else:
                            pe.quiet(issue, r_ok, acc_free)
                tmp.give(r, mm2)
                yield
            tmp.give(hT, mm)
            x_ok = dve.do(op("tensor_tensor", xb[i], hv2, xb[i], ALU.add), mm2, s_ok)
            banks1.give(acc, x_ok)
            sent = x_sent[i].load(sp, x_dram[0][b].rearrange("t p d -> p t d"), xb[i], x_ok)
            S["x_sent"][b] = sent
            S["x_new"] = x_ok
            yield

        def back_and_gate(b):
            yield from mamba_back(b)
            give = lambda mark: load_x(b + 2, mark, S["x_sent"][b]) if b + 2 < NB else None
            yield from gate_step(b, xb[b % 2], S["x_new"], give, banks1, tmp, state, xwo_sent, xwo_dram[0])

        def others(b):
            if b >= 1:
                yield from back_and_gate(b - 1)
            if b + 1 < NB:
                yield from mamba_front(b + 1)

        load_x(1)
        weave((mamba_front(0), 1))
        for b in range(NB):
            weave((mamba_scan(b), 20), (others(b), 55 if 0 < b < NB - 1 else 27))
        weave((back_and_gate(NB - 1), 1))

        def final_state(tmp, banks, uo_free=None):
            ps, pf = banks.take()
            hv = halves(ps)
            mm = product([(hv[:, t, :], [(c_state[:, k, t * P:(t + 1) * P], uo[:, k, :]) for k in range(NF)]) for t in range(NT)],
                         state["c"], pf)
            return ps, hv, mm

        ps, hv, mm = final_state(tmp, banks1)
        everything = [(x.sem, x.count) for x in (act, dve, pool, pe)] + [(a.sem, a.count) for a in
                     [*x_sent, *xwo_sent, dd_sent, *dd_in, *bc_sent, *bc_in]]

        top[0] = shared_top
        w_v = sb(NF, D)
        w_o = sb(NF, D)
        w_q = sb(NF, P)
        cuo = sb(NT, D)
        x2 = [sb(NT, D) for _ in range(3)]
        qp = [sb(HU, L, dt=BF16) for _ in range(3)]
        kp = [sb(HU, L, dt=BF16) for _ in range(3)]
        parts = [sb(3, NF, L, dt=BF16) for _ in range(2)]
        v_sb = [sb(NT, NH, VW) for _ in range(2)]
        p_ring = Ring([sb(L) for _ in range(10)])
        ot = [sb(2, L) for _ in range(2)]
        on = sb(NT, HU * HD)
        oT = sb(NF, L)
        mx = [sb(HU * NT) for _ in range(2)]
        nm = sb(P)
        nm_parts = sb(3, P, dt=BF16)
        rden = sb(NT, HU)
        tmp2 = Ring([sb(NT * D) for _ in range(8)])
        qk_rows = {"q": [0, 0, 1, 1, 0, 2], "k": [0, 1, 0, 1, 2, 0]}
        nrow = 6 * HD

        w_att.load(sp, w_v, kn(t_in["w_v"]), everything)
        w_att.load(sp, w_o, kn(t_in["w_o"]))
        att_ready = w_att.load(sp, w_q, t_in["w_q"].rearrange("p (f m) -> p f m", f=NF))

        cuo_ok = dve.do(op("tensor_copy", cuo, hv), mm, everything)
        state["c"] = start_state(mm)
        for i in range(2):
            v_set = pool.do(op("memset", v_sb[i], 0.0), everything)
        for i in range(2):
            v_set = pool.do(op("memset", v_sb[i][:, :, :, HD:HD + 1], 1.0), v_set)
        for i in range(3):
            k_ones = dve.do(op("memset", kp[i][nrow:nrow + 3], 1.0), everything)

        max_banks = Ring([bank(0), bank(1)])
        st_banks = Ring([bank(2), bank(3)])
        pv_banks = Ring([bank(4), bank(5)])
        banks2 = Ring([pair(3)])
        for ring in (max_banks, st_banks, pv_banks, banks2):
            ring.items = [(x, list(everything) + [cuo_ok]) for x, _ in ring.items]
        p_ring.items = [(x, everything) for x, _ in p_ring.items]
        tmp2.items = [(x, everything) for x, _ in tmp2.items]

        x2_in, xwo_in = [arrive(f"x2_in{i}") for i in range(2)], [arrive(f"xwo_in{i}") for i in range(2)]
        part_sent = [arrive(f"part_sent{i}") for i in range(2)]
        qk_in = [arrive(f"qk_in{i}") for i in range(3)]
        nm_sent, nm_in = arrive("max_sent"), [arrive(f"max_in{i}") for i in range(3)]
        x3_sent = [arrive(f"x3_sent{i}") for i in range(2)]
        xwo2_sent = [arrive(f"xwo2_sent{i}") for i in range(2)]
        state["sent"] = []
        T = {"x2": {}, "x2_free": [everything] * 3, "parts_free": [everything, everything], "v": {}, "v_free": [everything] * 2,
             "qk_free": [everything] * 3, "qk": {}, "part": {}, "part_read": {}, "nm": {}, "nm_free": everything,
             "nm_read": {}, "ot_free": [everything] * 2, "on_free": everything, "oT_free": everything, "mx_free": [everything] * 2,
             "x3": {}, "x_sent": {}, "rden_free": everything}

        def attend_front(b):
            i, i3 = b % 2, b % 3
            xs, fs = yield from grab(tmp2)
            xw, fw = yield from grab(tmp2)
            xs_ok = x2_in[i].load(sp, tok(xs), x_dram[0][b].rearrange("t p d -> p t d"), fs)
            xw_ok = xwo_in[i].load(sp, tok(xw), xwo_dram[0][b].rearrange("t p d -> p t d"), fw)
            yield
            a = pool.do(op("tensor_tensor", tok(xw), tok(xw), cuo, ALU.add), xw_ok, cuo_ok)
            a = act.do(op("activation", xw, xw, ACT.Tanh), a)
            yield
            x2_ok = pool.do(op("tensor_tensor", x2[i3], tok(xs), tok(xw), ALU.add), a, xs_ok, T["x2_free"][i3])
            tmp2.give(xs, x2_ok)
            tmp2.give(xw, x2_ok)
            yield
            xa, fa = yield from grab(tmp2)
            xa_ok = normalise(x2[i3], tok(xa), x2_ok, 0, fa)
            T["x2"][b] = pool.do(op("tensor_tensor", x2[i3], x2[i3], over_tiles(row("out_b")), ALU.add), xa_ok)
            yield
            ps, pf = yield from grab(banks2)
            turned = turn(tok(xa), xa_ok, ps, pf)
            tmp2.give(xa, turned)
            xaT, fx = yield from grab(tmp2)
            yield
            k_ok = dve.do(op("tensor_copy", feat(xaT), ps), turned, fx)
            banks2.give(ps, k_ok)
            ps, pf = yield from grab(banks2)
            mm = product([(ps[:, f, :], [(w_q[:, f, :], feat(xaT)[:, f, :])]) for f in range(NF)], k_ok, pf, att_ready)
            q, fq = yield from grab(tmp2)
            yield
            q_ok = act.do(op("activation", feat(q), ps, ACT.Copy), mm, fq)
            banks2.give(ps, q_ok)
            ps, pf = yield from grab(banks2)
            hv = halves(ps)
            mm = product([(hv[:, t, :], [(feat(xaT)[:, k, t * P:(t + 1) * P], w_v[:, k, :]) for k in range(NF)]) for t in range(NT)],
                         k_ok, pf)
            yield
            bv = over_tiles(row("wv_b")).rearrange("p t (h e) -> p t h e", e=HD)
            for t in range(NT):
                v_ok = dve.do(op("tensor_tensor", v_sb[i][:, t, :, 0:HD], hv[:, t, :].rearrange("p (h e) -> p h e", e=HD),
                              row("wv_b").rearrange("p (h e) -> p h e", e=HD), ALU.add), mm, v_set, T["v_free"][i])
            T["v"][b] = v_ok
            banks2.give(ps, v_ok)
            yield
            for n, (src, ok) in enumerate([(q, q_ok), (xaT, k_ok)]):
                pt = parts[n]
                r, fr = yield from grab(tmp2)
                a = dve.do(op("tensor_copy", pt[:, 0, :, :], feat(src)), ok, T["parts_free"][n])
                a = pool.do(op("tensor_tensor", feat(r), feat(src), pt[:, 0, :, :], ALU.subtract), a, fr)
                yield
                a = dve.do(op("tensor_copy", pt[:, 1, :, :], feat(r)), a)
                a = pool.do(op("tensor_tensor", pt[:, 2, :, :], feat(r), pt[:, 1, :, :], ALU.subtract), a)
                yield
                tmp2.give(r, a)
                tmp2.give(src, a, mm)
                sent = None
                for c in range(3):
                    sent = part_sent[i].load(sp, part_dram[i][n, c].rearrange("(f p) t -> p f t", p=P), pt[:, c], a, T["part_read"].get(b - 2))
                T["parts_free"][n] = sent
            T["part"][b] = sent
            yield

        def fetch_qk(u):
            b, f, s = u // 2, u % 2, u % 3
            for n, (name, dst) in enumerate([("q", qp[s]), ("k", kp[s])]):
                for r, c in enumerate(qk_rows[name]):
                    got = qk_in[s].load(sp, dst[r * HD:(r + 1) * HD],
                                        part_dram[b % 2][n, c, f * P:(f + 1) * P, :].rearrange("(h e) t -> e h t", e=HD),
                                        T["part"][b], T["qk_free"][s])
            T["qk"][u] = got
            if f == 1:
                T["part_read"][b] = [T["qk"][u - 1], got]

        def attend_max(u):
            s, m = u % 3, mx[u % 2]
            for h in range(HU):
                for t in range(NT):
                    ps, pf = max_banks.take()
                    mm = product([(ps, [(qp[s][0:nrow, h, t * P:(t + 1) * P], kp[s][0:nrow, h, :])])], T["qk"][u], pf)
                    m_ok = dve.do(op("tensor_reduce", m[:, h * NT + t:h * NT + t + 1], ps, AXIS.X, ALU.max),
                                  mm, T["mx_free"][u % 2])
                    max_banks.give(ps, m_ok)
                yield
            ps, pf = max_banks.take()
            n = HU * NT
            turned = pe.do(op("transpose", ps[0:n, 0:P], m, ident), m_ok, pf)
            T["mx_free"][u % 2] = turned
            a = dve.do(op("tensor_scalar", nm[0:n, :], ps[0:n, 0:P], -1.0, None, ALU.mult), turned, T["nm_free"])
            max_banks.give(ps, a)
            for c in range(3):
                a = dve.do(op("tensor_copy", nm_parts[0:n, c, :], nm[0:n, :]), a, T["nm_free"])
                if c < 2:
                    a = dve.do(op("tensor_tensor", nm[0:n, :], nm[0:n, :], nm_parts[0:n, c, :], ALU.subtract), a)
            sent = nm_sent.load(sp, max_dram[u % 2].rearrange("c r t -> r c t"), nm_parts[0:n], a, T["nm_read"].get(u - 2))
            T["nm_free"] = sent
            T["nm"][u] = nm_in[s].load(sp, qp[s][nrow:nrow + 3, :, :], max_dram[u % 2].rearrange("c (h r) t -> c h (r t)", h=HU), sent)
            T["nm_read"][u] = T["nm"][u]
            yield

        def attend_exp(u):
            b, f, s = u // 2, u % 2, u % 3
            vb = v_sb[b % 2]
            o_u = ot[u % 2]
            for q in range(2):
                pv, pv_free = pv_banks.take()
                waiting = []

                def values(held):
                    kt, ps_ = held
                    for hh, (pt, p_ok) in enumerate(ps_):
                        issue = op("matmul", pv[hh * VW:(hh + 1) * VW, :],
                                vb[:, kt, f * HU + q * 4 + hh, :], pt, start=kt == 0, stop=kt == NT - 1)
                        if hh == 3:
                            ok = pe.do(issue, p_ok)
                        else:
                            pe.quiet(issue, [p for _, p in ps_], pv_free, T["v"][b])
                    for pt, _ in ps_:
                        p_ring.give(pt, ok)
                    return ok
                for kt in range(NT):
                    held = []
                    for hh in range(4):
                        h = q * 4 + hh
                        st, sf = st_banks.take()
                        mm = product([(st, [(kp[s][0:nrow + 3, h, kt * P:(kt + 1) * P], qp[s][0:nrow + 3, h, :])])],
                                     T["nm"][u], T["qk"][u], k_ones, sf)
                        pt, pf = p_ring.take()
                        p_ok = act.do(op("activation", pt, st, ACT.Exp, scale=HD ** -0.5), mm, pf)
                        st_banks.give(st, p_ok)
                        held.append((pt, p_ok))
                        if hh == 1 and waiting:
                            ok = values(waiting.pop())
                    waiting.append((kt, held))
                    yield
                ok = values(waiting.pop())
                ot_ok = dve.do(op("tensor_copy", o_u[:, q, :], pv), ok, T["ot_free"][u % 2])
                pv_banks.give(pv, ot_ok)
                yield
            T["qk_free"][s] = mm
            if f == 1:
                T["v_free"][b % 2] = ok
            yield
            ps, pf = yield from grab(banks2)
            pv4 = ps.rearrange("p b (u r) -> p (b u) r", u=NT // 2)
            for t in range(NT):
                for q in range(2):
                    issue = op("transpose", pv4[:, t, q * P:(q + 1) * P], o_u[:, q, t * P:(t + 1) * P], ident)
                    if t == NT - 1 and q == 1:
                        turned = pe.do(issue, ot_ok, pf)
                    else:
                        pe.quiet(issue, ot_ok, pf)
            T["ot_free"][u % 2] = turned
            yield
            p5 = pv4.rearrange("p t (h e) -> p t h e", e=VW)
            r_ok = dve.do(op("reciprocal", rden.unsqueeze(3), p5[:, :, :, HD:HD + 1]), turned, T["rden_free"])
            for t in range(NT):
                on_ok = dve.do(op("tensor_tensor", on[:, t, :].rearrange("p (h e) -> p h e", e=HD), p5[:, t, :, 0:HD],
                               rden[:, t, :].unsqueeze(2).to_broadcast([P, HU, HD]), ALU.mult), r_ok, T["on_free"])
            T["rden_free"] = on_ok
            banks2.give(ps, on_ok)
            yield
            ps, pf = yield from grab(banks2)
            for t in range(NT):
                issue = op("transpose", ps[:, 0, t * P:(t + 1) * P], on[:, t, :], ident)
                if t == NT - 1:
                    turned = pe.do(issue, on_ok, pf)
                else:
                    pe.quiet(issue, on_ok, pf)
            T["on_free"] = turned
            yield
            oT_ok = act.do(op("activation", oT[:, f, :], ps[:, 0, :], ACT.Copy), turned, T["oT_free"] if f == 0 else None)
            banks2.give(ps, oT_ok)
            if f == 0:
                T["oT_half"] = oT_ok
                return
            ps, pf = yield from grab(banks2)
            hv = halves(ps)
            mm = product([(hv[:, t, :], [(oT[:, k, t * P:(t + 1) * P], w_o[:, k, :]) for k in range(NF)]) for t in range(NT)],
                         oT_ok, T["oT_half"], pf)
            T["oT_free"] = mm
            i3 = b % 3
            yield
            x3_ok = dve.do(op("tensor_tensor", x2[i3], hv, x2[i3], ALU.add), mm, T["x2"][b])
            banks2.give(ps, x3_ok)
            T["x3"][b] = x3_ok
            T["x_sent"][b] = x3_sent[b % 2].load(sp, x_dram[1][b].rearrange("t p d -> p t d"), x2[i3], x3_ok)

        def second_gate(b):
            def give(mark):
                T["x2_free"][b % 3] = [mark, T["x_sent"][b]]
            yield from gate_step(b, x2[b % 3], T["x3"][b], give, banks2, tmp2, state, xwo2_sent, xwo_dram[1])

        NU = 2 * NB
        weave((attend_front(0), 1))
        fetch_qk(0)
        fetch_qk(1)
        weave((attend_max(0), 1))
        for u in range(NU):
            b, f = u // 2, u % 2
            streams = [(attend_exp(u), 17)]
            if u + 1 < NU:
                streams.append((attend_max(u + 1), 11))
            if f == 0 and b + 1 < NB:
                streams.append((attend_front(b + 1), 13))
            if f == 1 and b >= 1:
                streams.append((second_gate(b - 1), 15))
            weave(*streams)
            if f == 0 and u + 2 < NU:
                fetch_qk(u + 2)
                fetch_qk(u + 3)
        weave((second_gate(NB - 1), 1))

        ps, hv, mm = final_state(tmp2, banks2)
        cuo_ok = dve.do(op("tensor_copy", cuo, hv), mm)
        out_sent = [arrive(f"out_sent{i}") for i in range(2)]
        x3_in, xwo2_in = [arrive(f"x3_in{i}") for i in range(2)], [arrive(f"xwo2_in{i}") for i in range(2)]
        last = []
        for b in range(NB):
            i = b % 2
            xs, fs = tmp2.take()
            xw, fw = tmp2.take()
            xs_ok = x3_in[i].load(sp, tok(xs), x_dram[1][b].rearrange("t p d -> p t d"), fs, T["x_sent"][b])
            xw_ok = xwo2_in[i].load(sp, tok(xw), xwo_dram[1][b].rearrange("t p d -> p t d"), fw, state["sent"][b])
            a = (dve if b % 2 else pool).do(op("tensor_tensor", tok(xw), tok(xw), cuo, ALU.add), xw_ok, cuo_ok)
            a = act.do(op("activation", xw, xw, ACT.Tanh), a)
            a = dve.do(op("tensor_tensor", xs, xs, xw, ALU.add), a, xs_ok)
            sent = out_sent[i].load(sp, out[b].rearrange("(t p) d -> p t d", p=P), tok(xs), a)
            tmp2.give(xs, sent)
            tmp2.give(xw, a)
            last.append(sent)
        finals = last + [(a.sem, a.count) for a in [*x3_sent, *xwo2_sent, nm_sent, *part_sent]]

        block = ctx.enter_context(nc.Block())

        @block.sync
        def _(e):
            sp.emit(e)
            for s, v in sp.waits(finals):
                e.wait_ge(s, v)

        @block.scalar
        def _(e):
            act.emit(e)

        @block.vector
        def _(e):
            dve.emit(e)

        @block.gpsimd
        def _(e):
            pool.emit(e)

        @block.tensor
        def _(e):
            pe.emit(e)


def kernel(**inputs):
    import concourse.bacc as bacc
    from concourse.bass_utils import run_bass_kernel_spmd

    z = {k: np.asarray(v) for k, v in inputs.items()}
    a = lambda n: z["L0_attn_a_" + n]
    f = lambda n: z["L0_ffn_" + n]
    g = lambda n: z["L0_attn_b_" + n]
    cols = lambda v: v.reshape(-1, P).T
    conv = a("conv_w").reshape(NF, P, TAPS).transpose(1, 0, 2).reshape(P, NF * TAPS)
    a_log = a("A_log").reshape(NJ, EB, SG, NS // SG).transpose(2, 1, 0, 3).reshape(P, NJ * NS // SG)
    vec = np.concatenate([cols(a("ln2_g")), cols(a("ln2_b")), cols(a("rms_w")), conv, cols(a("conv_b")), cols(a("dt_proj_b")),
                          cols(a("D_param")), cols(a("ffn_b1")), cols(f("bf")), cols(f("bi")), cols(f("bc")), cols(f("in_c")),
                          a_log], axis=1)
    rows = np.stack([a("ln1_g"), a("ln1_b"), a("ffn_b2"), f("bo"), g("wv_b"), g("out_b")])
    w_q = np.zeros((P, NF, P), np.float32)
    for h in range(NH):
        r = h % HU * HD
        w_q[r:r + HD, h // HU, r:r + HD] = g("w_att_val")[h]
    sel = np.tile(np.eye(EB, dtype=np.float32), (SG, 1))
    arrays = {
        "x": a("x"), "vec": vec, "ident": np.eye(P, dtype=np.float32), "sel": sel, "rows": rows,
        "w_in": a("in_proj_w"), "w_xp": a("x_proj_w"), "w_dt": a("dt_proj_w"), "w_out": a("out_proj_w"),
        "w1": a("ffn_w1"), "w2": a("ffn_w2"),
        "wx": np.concatenate([f("wf").T, f("wi").T, f("wc").T], axis=1),
        "uh": np.concatenate([f("uf").T, f("ui").T, f("uc").T], axis=1),
        "wo": f("wo").T, "uo": f("uo").T, "w_v": g("wv_w").T, "w_o": g("out_w").T, "w_q": w_q.reshape(P, NF * P),
    }
    nc = bacc.Bacc("TRN2", target_bir_lowering=False, num_devices=1)
    feed, t_in = {}, {}
    for name, v in arrays.items():
        feed[f"{name}_dram"] = np.ascontiguousarray(v)
        t_in[name] = nc.dram_tensor(f"{name}_dram", v.shape, F32, kind="ExternalInput").ap()
    out = nc.dram_tensor("out_dram", (NB, L, D), F32, kind="ExternalOutput").ap()
    build(nc, t_in, out)
    r = run_bass_kernel_spmd(nc, [feed], core_ids=[0])
    return r.results[0]["out_dram"]
```

```python
import numpy as np
import concourse.bass as bass
from concourse import mybir
from contextlib import ExitStack

F32 = mybir.dt.float32
BF16 = mybir.dt.bfloat16
ALU = mybir.AluOpType
ACT = mybir.ActivationFunctionType
AXIS = mybir.AxisListType

P = 128
D = 256
NB, L = 8, 512
NT = L // P
NF = D // P
NS = 16
SG = 4
EB = P // SG
NJ = D // EB
TAPS = 4
RANK = 64
HID = 4 * D
NH, HD = 16, 16
HU = NH // 2
VW = 32
EPS = 1e-5

VEC = {}
for _n, _w in [("ln2_g", 2), ("ln2_b", 2), ("rms_w", 2), ("conv_w", 8), ("conv_b", 2), ("dt_b", 2),
               ("D", 2), ("ffn_b1", 8), ("bf", 2), ("bi", 2), ("bc", 2), ("in_c", 2), ("A_log", 32)]:
    VEC[_n] = (sum(w for _, w in VEC.values()), _w)
NVEC = sum(w for _, w in VEC.values())
ROWS = ["ln1_g", "ln1_b", "ffn_b2", "bo"]
ATT_ROWS = ["wv_b", "out_b"]


OPS = {
    "activation": lambda e: e.activation, "bn_stats": lambda e: e.bn_stats, "bn_aggr": lambda e: e.bn_aggr,
    "dma_start": lambda e: e.dma_start, "matmul": lambda e: e.matmul, "memset": lambda e: e.memset,
    "reciprocal": lambda e: e.reciprocal, "scalar_tensor_tensor": lambda e: e.scalar_tensor_tensor,
    "tensor_copy": lambda e: e.tensor_copy, "tensor_reduce": lambda e: e.tensor_reduce,
    "tensor_scalar": lambda e: e.tensor_scalar, "tensor_tensor": lambda e: e.tensor_tensor,
    "tensor_tensor_reduce": lambda e: e.tensor_tensor_reduce, "tensor_tensor_scan": lambda e: e.tensor_tensor_scan,
    "transpose": lambda e: e.transpose,
}


def marks(after):
    for mark in after:
        if isinstance(mark, list):
            yield from marks(mark)
        elif mark is not None:
            yield mark


def op(name, *operands, **modes):
    return name, operands, modes


def size(ap):
    return int(np.prod(ap.shape[1:]))


def estimate(name, operands, modes):
    if name in ("matmul", "transpose"):
        if name == "transpose":
            return 160
        stationary, moving = operands[1], operands[2]
        columns = size(moving) * (4 if moving.dtype is F32 else 1)
        return max(columns / (8.0 if size(stationary) == VW and moving.dtype is F32 else 2.4) + 5, 50)
    n = size(modes["in0"] if name == "tensor_tensor_reduce" else operands[1] if name in ("tensor_reduce", "bn_stats") else operands[0])
    if name == "activation":
        return n / 1.2 + 93 + 93 * sum(not isinstance(modes.get(m, 0), (int, float)) for m in ("bias", "scale"))
    if name in ("tensor_scalar", "tensor_copy"):
        return n / 1.92 + 68
    if name == "reciprocal":
        return 8 * n / 0.96 + 68
    return n / 0.96 + 68


class Step:

    def __init__(self, queue, issues, after, sem, by):
        self.queue, self.issues, self.after, self.sem, self.by = queue, issues, after, sem, by

    def start(self):
        return max([self.queue.free] + [Queue.due.get(m, 0.0) for m in marks(self.after)])

    def now(self):
        q = self.queue
        need = q.waits(self.after)
        for s, v in need:
            q.passed[s] = v
        start = self.start()
        if self.sem is q:
            q.free = start + sum(max(estimate(*issue) * q.slow, 0.0) for issue in self.issues)
            land = q.free + 60
        else:
            name, (out, _), _ = self.issues[0]
            q.free = start + 60
            Arrival.free = max(Arrival.free, start) + max(450.0, size(out) * out.shape[0] * (2 if out.dtype is BF16 else 4) / 200)
            land = Arrival.free + 2000
        for i, issue in enumerate(self.issues):
            last = i == len(self.issues) - 1
            q.steps.append((need if i == 0 else [], issue, self.sem.sem if last else None, self.by))
        self.sem.count += self.by
        Queue.due[self.sem.sem, self.sem.count] = land
        return (self.sem.sem, self.sem.count)


class Queue:

    due = {}

    def __init__(self, sem, slow=1.0):
        self.sem, self.count, self.passed, self.steps = sem, 0, {}, []
        self.free, self.slow = 0.0, slow

    def waits(self, after):
        need = {}
        for mark in marks(after):
            s, v = mark
            if v > self.passed.get(s, 0):
                need[s] = max(need.get(s, 0), v)
        return list(need.items())

    def do(self, issue, *after):
        return Step(self, [issue], after, self, 1)

    def group(self, issues, *after):
        return Step(self, issues, after, self, 1)

    def emit(self, eng):
        for need, issue, sem, by in self.steps:
            for s, v in need:
                eng.wait_ge(s, v)
            name, operands, modes = issue
            ins = OPS[name](eng)(*operands, **modes)
            if sem is not None:
                ins.then_inc(sem, by)


class Arrival:

    free = 0.0

    def __init__(self, sem):
        self.sem, self.count = sem, 0

    def load(self, queue, out, in_, *after):
        return Step(queue, [op("dma_start", out, in_)], after, self, 16)


class Ring:

    def __init__(self, items):
        self.items = [(x, None) for x in items]

    def take(self):
        return self.items.pop(0)

    def give(self, item, *marks):
        self.items.append((item, list(marks)))


WAIT = "wait"


def grab(ring):
    while not ring.items:
        yield WAIT
    return ring.take()


def until(there):
    while not there():
        yield WAIT


class Stream:

    def __init__(self, steps):
        self.steps, self.step, self.over = steps, WAIT, False

    def go(self, mark=None):
        try:
            self.step = self.steps.send(mark)
        except StopIteration:
            self.over = True


def weave(*streams):
    live = [Stream(g) for g in streams]
    while live:
        moved = True
        while moved:
            moved = False
            for s in live:
                if s.step is WAIT:
                    s.go()
                    moved = moved or s.step is not WAIT or s.over
            live = [s for s in live if not s.over]
        if live:
            ready = [s for s in live if s.step is not WAIT]
            assert ready, "every stream waits for another"
            s = min(ready, key=lambda x: x.step.start())
            s.go(s.step.now())
            live = [s for s in live if not s.over]


def build(nc, t_in, out):
    ctx = ExitStack()
    with ctx:
        sem = lambda name: ctx.enter_context(nc.semaphore(name))
        Queue.due, Arrival.free = {}, 0.0
        pe, act, dve, sp = (Queue(sem(n)) for n in ("pe_done", "act_done", "dve_done", "sp_done"))
        pool = Queue(sem("pool_done"), 2.1)
        arrive = lambda name: Arrival(sem(name))

        ARENA = 53180
        arena = ctx.enter_context(nc.sbuf_tensor("arena", [P, ARENA], F32))
        top = [0]

        def sb(*shape, dt=F32):
            n = int(np.prod(shape))
            words = n if dt is F32 else (n + 1) // 2
            at = top[0]
            top[0] += words
            assert top[0] <= ARENA, (top[0], ARENA)
            v = arena[:, at:at + words]
            if dt is not F32:
                v = v.bitcast(dt)
            if len(shape) > 1:
                names = " ".join(f"d{i}" for i in range(len(shape)))
                v = v.rearrange(f"p ({names}) -> p {names}",
                                **{f"d{i}": s for i, s in enumerate(shape)})
            return v

        psum = ctx.enter_context(nc.psum_tensor("psum", [P, 8, L], F32))
        bank = lambda i: psum[:, i, :]
        pair = lambda i: psum[:, 2 * i:2 * i + 2, :]

        dram = lambda name, shape, dt: nc.dram_tensor(name, shape, dt, kind="Internal").ap()
        dd_dram = [dram(f"dd{i}", (D, 2, L), F32) for i in range(2)]
        bc_dram = [dram(f"bc{i}", (2 * NS, L), F32) for i in range(2)]
        xh_dram = [dram(f"xh{i}", (NT, P, D), F32) for i in range(4)]
        part_dram = [dram(f"parts{i}", (2, 3, D, L), BF16) for i in range(2)]
        max_dram = [dram(f"max{i}", (3, HU * NT, P), BF16) for i in range(2)]
        x_dram = [dram(f"x_after_{n}", (NB, NT, P, D), F32) for n in ("mamba", "attention")]
        xwo_dram = [dram(f"xwo_{n}", (NB, NT, P, D), F32) for n in ("first", "second")]

        ident = sb(P)
        sel = sb(EB)
        vec = sb(NVEC)
        rows = sb(len(ROWS), D)
        wx = sb(NF, 3 * D)
        uh = sb(NF, 3 * D)
        wo = sb(NF, D)
        uo = sb(NF, D)
        half_bias = sb(4)
        conv_half = sb(10)
        A_neg = sb(NJ * SG)
        c_state = sb(NF, L)
        stats = [sb(NT, 6) for _ in range(2)]
        mv = [sb(NT, 2) for _ in range(2)]
        rstd = [sb(NT) for _ in range(2)]
        neg_half = sb(NT)
        col = lambda name, i=0: vec[:, VEC[name][0] + i:VEC[name][0] + i + 1]
        row = lambda name: rows[:, ROWS.index(name), :]
        over_tiles = lambda r: r.unsqueeze(1).to_broadcast([P, NT, D])
        shared_top = top[0]

        w_small, w_mamba, w_ffn, w_gate, w_att = (arrive(f"weights_{n}") for n in
                                                  ("small", "mamba", "ffn", "gate", "attention"))
        x_in = [arrive(f"x_in{i}") for i in range(2)]
        kn = lambda ap: ap.rearrange("(k p) n -> p k n", p=P)

        w_in = sb(NF, 2 * D)
        w_xp = sb(NF, RANK + 2 * NS)
        w_dt = sb(D)
        w_out = sb(NF, D)
        w1 = sb(NF, HID)
        w2 = sb(HID // P, D)
        x_front = sb(NT, D)
        x_back = sb(NT, D)
        xh_back = sb(NT, D)
        xi_pad = sb(NF, TAPS - 1 + L)
        xc = [sb(NF, L) for _ in range(2)]
        sz = [sb(NF, L) for _ in range(2)]
        dbc = sb(L)
        dd_out = sb(NF, 2, L)
        NSLOT = 6
        ddb = sb(NSLOT, 2, L)
        bcb = [sb(2, 2, L) for _ in range(2)]
        dA_ring = Ring([sb(2, L) for _ in range(3)])
        hb_ring = Ring([sb(2, L) for _ in range(5)])
        tmp = Ring([sb(NT * D) for _ in range(3)])
        tmp_middle = Ring([sb(NT * D) for _ in range(2)])
        tmp_back = Ring([sb(NT * D) for _ in range(2)])
        tmp_gate = Ring([sb(NT * D) for _ in range(4)])
        tok = lambda v: v.rearrange("p (t d) -> p t d", t=NT)
        feat = lambda v: v.rearrange("p (f t) -> p f t", f=NF)

        load = w_small.load
        load(sp, vec, t_in["vec"]).now()
        load(sp, ident, t_in["ident"]).now()
        load_x = lambda b, *after: x_in[b % 2].load(sp, x_front, t_in["x"][b].rearrange("(t p) d -> p t d", p=P), *after)
        x_loads, x_left = {0: load_x(0).now()}, {}
        load(sp, sel, t_in["sel"]).now()
        small_ready = load(sp, rows, t_in["rows"].partition_broadcast(P)).now()
        w_mamba.load(sp, w_in, kn(t_in["w_in"])).now()
        w_mamba.load(sp, w_xp, kn(t_in["w_xp"])).now()
        w_mamba.load(sp, w_dt[0:RANK, :], t_in["w_dt"]).now()
        mamba_ready = w_mamba.load(sp, w_out, kn(t_in["w_out"])).now()
        w_ffn.load(sp, w1, kn(t_in["w1"])).now()
        ffn_ready = w_ffn.load(sp, w2, kn(t_in["w2"])).now()
        w_gate.load(sp, wx, kn(t_in["wx"])).now()
        w_gate.load(sp, uh, kn(t_in["uh"])).now()
        w_gate.load(sp, wo, kn(t_in["wo"])).now()
        gate_ready = w_gate.load(sp, uo, kn(t_in["uo"])).now()

        c0 = VEC["bf"][0]
        made_bias = dve.do(op("tensor_scalar", half_bias, vec[:, c0:c0 + 4], 0.5, None, ALU.mult), small_ready).now()
        c1 = VEC["conv_w"][0]
        made_conv = dve.do(op("tensor_scalar", conv_half, vec[:, c1:c1 + 10], 0.5, None, ALU.mult)).now()
        c2 = VEC["A_log"][0]
        exp_A = act.do(op("activation", A_neg, vec[:, c2:c2 + NJ * SG], ACT.Exp), small_ready).now()
        made_A = dve.do(op("tensor_scalar", A_neg, A_neg, -1.0, None, ALU.mult), exp_A).now()
        minus_half = pool.do(op("memset", neg_half, -0.5)).now()
        zero_pad = pool.do(op("memset", xi_pad[:, :, 0:TAPS - 1], 0.0)).now()

        def start_state(*after):
            z = dve.do(op("memset", c_state, 0.0), *after).now()
            for f in range(NF):
                z0 = z
                z = dve.do(op("tensor_scalar", c_state[:, f, :], c_state[:, f, :], col("in_c", f), None, ALU.add), z0, small_ready).now()
            return z

        def normalise(src, dst, ready, which, free=None):
            st, m, r = stats[which], mv[which], rstd[which]
            for t in range(NT):
                a = yield dve.do(op("bn_stats", st[:, t, :], src[:, t, :]), ready)
            for t in range(NT):
                b_ = yield dve.do(op("bn_aggr", m[:, t, :], st[:, t, :]), a)
            c = yield dve.do(op("tensor_scalar", r.unsqueeze(2), m[:, :, 1:2], EPS, None, ALU.add), b_)
            c = yield pool.do(op("tensor_tensor", r, r, neg_half, ALU.pow), c, minus_half)
            for t in range(NT):
                d_ = yield dve.do(op("tensor_scalar", dst[:, t, :], src[:, t, :], m[:, t, 0:1], r[:, t:t + 1],
                                                           ALU.subtract, ALU.mult), c, free)
            return d_

        def turn(src, ready, to, free):
            return pe.group([op("transpose", to[:, f, t * P:(t + 1) * P], src[:, t, f * P:(f + 1) * P], ident)
                             for f in range(NF) for t in range(NT)], ready, free, small_ready)

        def product(outs, *after):
            for o, terms in outs:
                done = yield pe.group([op("matmul", o, l, r, start=k == 0, stop=k == len(terms) - 1)
                                       for k, (l, r) in enumerate(terms)], *after)
            return done

        def halves(v):
            return v.rearrange("p b (u d) -> p (b u) d", u=NT // 2)

        def gate_step(b, x_new, ready, x_give, banks, tmp, state, xwo_arrive, xwo_out):
            xr, free = yield from grab(tmp)
            xr_done = yield from normalise(x_new, tok(xr), ready, 1, free)
            x_give(xr_done)
            xrT, free = yield from grab(tmp)
            ps, ps_free = yield from grab(banks)
            turned = yield turn(tok(xr), xr_done, ps, ps_free)
            tmp.give(xr, turned)
            xrT_done = yield act.do(op("activation", feat(xrT), ps, ACT.Copy), turned, free)
            banks.give(ps, xrT_done)
            ps, ps_free = yield from grab(banks)
            hv = halves(ps)
            wo_done = yield from product([(hv[:, t, :], [(feat(xrT)[:, k, t * P:(t + 1) * P], wo[:, k, :]) for k in range(NF)])
                               for t in range(NT)], xrT_done, ps_free, gate_ready)
            xwo, free = yield from grab(tmp)
            xwo_done = yield dve.do(op("tensor_tensor", tok(xwo), hv, over_tiles(row("bo")), ALU.add), wo_done, free)
            banks.give(ps, xwo_done)
            xwo_sent = yield xwo_arrive[b % 2].load(sp, xwo_out[b].rearrange("t p d -> p t d"), tok(xwo), xwo_done)
            tmp.give(xwo, xwo_sent)
            state["sent"].append(xwo_sent)
            gates = []
            for g, (fn, sc) in enumerate([(ACT.Tanh, 0.5), (ACT.Tanh, 0.5), (ACT.Tanh, 1.0)]):
                ps, ps_free = yield from grab(banks)
                for f in range(NF):
                    w = slice(g * D + f * P, g * D + (f + 1) * P)
                    mm = yield from product([(ps[:, f, :], [(wx[:, k, w], feat(xrT)[:, k, :]) for k in range(NF)]
                                   + [(uh[:, k, w], c_state[:, k, :]) for k in range(NF)])],
                                 xrT_done, ps_free, gate_ready, state["c"])
                gt, free = yield from grab(tmp)
                for f in range(NF):
                    bias = half_bias[:, 2 * g + f:2 * g + f + 1] if g < 2 else col("bc", f)
                    done = yield act.do(op("activation", feat(gt)[:, f, :], ps[:, f, :], fn, bias=bias, scale=sc), mm, free, made_bias)
                banks.give(ps, done)
                gates.append((gt, done))
            tmp.give(xrT, mm)
            (gf, f_ok), (gi, i_ok), (gc, c_ok) = gates
            a = yield dve.do(op("scalar_tensor_tensor", feat(gf), feat(gf), 1.0, c_state, ALU.add, ALU.mult), f_ok, state["c"])
            d_ = yield dve.do(op("scalar_tensor_tensor", feat(gi), feat(gi), 1.0, feat(gc), ALU.add, ALU.mult), i_ok, c_ok)
            s = yield dve.do(op("tensor_tensor", gf, gf, gi, ALU.add), a, d_)
            state["c"] = yield dve.do(op("tensor_scalar", c_state, feat(gf), 0.5, None, ALU.mult), s, mm)
            for gt in (gf, gi, gc):
                tmp.give(gt, state["c"])

        cleared = [dve.do(op("memset", pair(i), 0.0)).now() for i in range(3)]
        banks1 = Ring([pair(0), pair(1), pair(2)])
        banks1.items = [(x, [m]) for (x, _), m in zip(banks1.items, cleared)]
        y_pair = pair(3)
        state = {"c": start_state(), "sent": []}
        bc_sent, bc_in = [arrive(f"bc_out{i}") for i in range(2)], [arrive(f"bc_in{i}") for i in range(2)]
        dd_sent, dd_in = arrive("dd_out"), [arrive(f"dd_in{i}") for i in range(NSLOT)]
        x_sent = [arrive(f"x_sent{i}") for i in range(2)]
        xwo_sent = [arrive(f"xwo_sent{i}") for i in range(2)]
        S = {"xc": {}, "sz": {}, "xh": {}, "xb2": {}, "dd": {}, "bc": {}, "y_free": [None] * NF, "scans": 0, "yT": {}, "du": {}, "fed": [], "scanned": [], "z": {}, "xi": {}, "convs": 0, "dd_read": {},
             "bc_read": {}, "xi_free": None, "dbc_free": None, "dd_out_free": None, "xc_free": [None, None],
             "sz_free": [None, None], "xh_free": [None, None], "ddb_free": [None] * NSLOT, "bcb_free": [None, None],
             "x_sent": {}, "bc_src": {}, "dd_src": {}, "bcb_freed": [-1, -1],
             "dd_loads": 0, "dd_used": 0, "backs": 0, "back_loads": 0, "outs": 0, "x_back_free": None, "xh_read": {}, "xh_back_free": None}

        xh_sent = [arrive(f"xh_sent{i}") for i in range(4)]
        back_in = arrive("back_in")

        def back_loads():
            for b in range(NB):
                yield from until(lambda: b in S["xh"] and S["backs"] == b)
                yield back_in.load(sp, x_back, t_in["x"][b].rearrange("(t p) d -> p t d", p=P), S["x_back_free"])
                S["x_back"] = yield back_in.load(sp, xh_back, xh_dram[b % 4].rearrange("t p d -> p t d"), S["xh"][b], S["xh_back_free"])
                S["xh_read"][b] = S["x_back"]
                S["back_loads"] = b + 1

        def x_fetches():
            for b in range(1, NB):
                yield from until(lambda: b - 1 in x_left)
                x_loads[b] = yield load_x(b, x_left[b - 1])

        def mamba_front(b):
            i = b % 2
            yield from until(lambda: b in x_loads)
            x_ok = x_loads[b]
            xn, f1 = yield from grab(tmp)
            xn_ok = yield from normalise(x_front, tok(xn), x_ok, 0, f1)
            x_left[b] = xn_ok
            h, f2 = yield from grab(tmp)
            h0_ok = yield from normalise(tok(xn), tok(h), xn_ok, 0, f2)
            hg_ok = yield pool.do(op("tensor_tensor", tok(h), tok(h), over_tiles(row("ln1_g")), ALU.mult), h0_ok, small_ready)
            h_ok = yield pool.do(op("tensor_tensor", tok(h), tok(h), over_tiles(row("ln1_b")), ALU.add), hg_ok)
            xh_ok = yield pool.do(op("tensor_tensor", tok(xn), tok(xn), tok(h), ALU.add), h_ok)
            S["xh"][b] = yield xh_sent[b % 4].load(sp, xh_dram[b % 4].rearrange("t p d -> p t d"), tok(xn), xh_ok, S["xh_read"].get(b - 4))
            mT, f3 = yield from grab(tmp)
            for t in range(NT):
                q = yield dve.do(op("tensor_tensor_reduce", out=tok(mT)[:, t, :], in0=tok(h)[:, t, :], in1=tok(h)[:, t, :],
                                    scale=1.0, scalar=0.0, op0=ALU.mult, op1=ALU.add,
                                    accum_out=rstd[0][:, t:t + 1]), h_ok, f3)
            q = yield dve.do(op("tensor_scalar", rstd[0], rstd[0], 1.0 / D, EPS, ALU.mult, ALU.add), q)
            q = yield pool.do(op("tensor_tensor", rstd[0], rstd[0], neg_half, ALU.pow), q)
            for t in range(NT):
                m_ok = yield dve.do(op("tensor_scalar", tok(h)[:, t, :], tok(h)[:, t, :], rstd[0][:, t:t + 1], None, ALU.mult),
                                    q, xh_ok)
            tmp.give(xn, S["xh"][b])
            ps, pf = yield from grab(banks1)
            turned = yield turn(tok(h), m_ok, ps, pf)
            tmp.give(h, turned)
            for f in range(NF):
                mT_ok = yield act.do(op("activation", feat(mT)[:, f, :], ps[:, f, :], ACT.Copy, scale=col("rms_w", f)), turned, q)
            banks1.give(ps, mT_ok)
            for part in range(2):
                ps, pf = yield from grab(banks1)
                mm = yield from product([(ps[:, f, :], [(w_in[:, k, part * D + f * P:part * D + (f + 1) * P], feat(mT)[:, k, :])
                                             for k in range(NF)]) for f in range(NF)], mT_ok, pf, mamba_ready)
                if part == 0:
                    yield from until(lambda: S["convs"] >= b)
                    xi_ok = yield act.do(op("activation", xi_pad[:, :, TAPS - 1:], ps, ACT.Copy), mm, S["xi_free"], zero_pad)
                    banks1.give(ps, xi_ok)
                else:
                    yield from until(lambda: S["outs"] >= b - 1)
                    z_ok = yield act.do(op("activation", sz[i], ps, ACT.Copy, scale=0.5), mm, S["sz_free"][i])
                    banks1.give(ps, z_ok)
            tmp.give(mT, mm)
            S["z"][b], S["xi"][b] = z_ok, xi_ok

        def mamba_middle(b):
            i = b % 2
            z_ok, xi_ok = S["z"][b], S["xi"][b]
            cv, fc = yield from grab(tmp_middle)
            for f in range(NF):
                w = lambda k, f=f: conv_half[:, f * TAPS + k:f * TAPS + k + 1]
                c_ok = yield dve.do(op("tensor_scalar", feat(cv)[:, f, :], xi_pad[:, f, TAPS - 1:], w(TAPS - 1),
                                                                  conv_half[:, 8 + f:9 + f], ALU.mult, ALU.add), xi_ok, fc, made_conv)
                for k in range(TAPS - 1):
                    c_ok = yield dve.do(op("scalar_tensor_tensor", feat(cv)[:, f, :], xi_pad[:, f, k:k + L], w(k),
                                                                                  feat(cv)[:, f, :], ALU.mult, ALU.add), c_ok)
            S["xi_free"] = c_ok
            S["convs"] = b + 1
            th, tz = dd_out[:, :, 0, :], dd_out[:, :, 1, :]
            th_ok = yield act.do(op("activation", th, feat(cv), ACT.Tanh), c_ok, S["dd_out_free"])
            tz_ok = yield act.do(op("activation", tz, sz[i], ACT.Tanh), z_ok, S["dd_out_free"])
            xc_ok = yield dve.do(op("scalar_tensor_tensor", xc[i], th, 1.0, feat(cv), ALU.add, ALU.mult), th_ok, S["xc_free"][i])
            tmp_middle.give(cv, xc_ok)
            S["sz"][b] = yield dve.do(op("scalar_tensor_tensor", sz[i], tz, 1.0, sz[i], ALU.add, ALU.mult), tz_ok)
            ps, pf = yield from grab(banks1)
            nr = RANK + 2 * NS
            mm = yield from product([(ps[0:nr, 0, :], [(w_xp[:, k, :], xc[i][:, k, :]) for k in range(NF)])], xc_ok, pf)
            dbc_ok = yield act.do(op("activation", dbc[0:nr, :], ps[0:nr, 0, :], ACT.Copy), mm, S["dbc_free"])
            banks1.give(ps, dbc_ok)
            sent = yield bc_sent[i].load(sp, bc_dram[i], dbc[RANK:nr, :], dbc_ok, S["bc_read"].get(b - 2))
            src = bc_dram[i].rearrange("(c s q g) t -> s q c g t", c=2, s=SG, q=2)
            ps, pf = yield from grab(banks1)
            mm = yield from product([(ps[:, f, :], [(w_dt[0:RANK, f * P:(f + 1) * P], dbc[0:RANK, :])]) for f in range(NF)], dbc_ok, pf)
            S["dbc_free"] = [mm, sent]
            S["bc_src"][b] = (src, sent)
            v, fv = yield from grab(tmp_middle)
            for f in range(NF):
                v_ok = yield act.do(op("activation", feat(v)[:, f, :], ps[:, f, :], ACT.Identity, bias=col("dt_b", f)), mm, fv)
            banks1.give(ps, v_ok)
            u, fu = yield from grab(tmp_middle)
            ln, w_ = dd_out[:, :, 0, :], dd_out[:, :, 1, :]
            a_ok = yield dve.do(op("scalar_tensor_tensor", u, v, -1.0, v, ALU.mult, ALU.min), v_ok, fu)
            u_ok = yield act.do(op("activation", u, u, ACT.Exp), a_ok)
            w_ok = yield dve.do(op("tensor_scalar", w_, feat(u), 1.0, -1.0, ALU.add, ALU.add), u_ok, S["sz"][b])
            ln_ok = yield act.do(op("activation", ln, feat(u), ACT.Ln, bias=1.0), u_ok, xc_ok)
            r_ok = yield dve.do(op("tensor_tensor", w_, feat(u), w_, ALU.subtract), w_ok)
            s_ok = yield dve.do(op("tensor_tensor", ln, ln, w_, ALU.add), r_ok, ln_ok)
            d_ok = yield dve.do(op("scalar_tensor_tensor", ln, feat(v), 0.0, ln, ALU.max, ALU.add), s_ok)
            tmp_middle.give(u, r_ok, ln_ok)
            tmp_middle.give(v, d_ok)
            S["du"][b] = du_ok = yield pool.do(op("tensor_tensor", dd_out[:, :, 1, :], dd_out[:, :, 0, :], xc[i], ALU.mult), d_ok)
            sent = yield dd_sent.load(sp, dd_dram[i].rearrange("(f p) c t -> p f c t", p=P), dd_out, d_ok, du_ok, S["dd_read"].get(b - 2))
            S["dd_out_free"] = sent
            S["dd_src"][b] = sent

        def bc_spread():
            for b in range(NB):
                for q in range(2):
                    yield from until(lambda: b in S["bc_src"] and S["bcb_freed"][q] == b - 1)
                    src, sent = S["bc_src"][b]
                    for s in range(SG):
                        got = yield bc_in[q].load(sp, bcb[q][s * EB:(s + 1) * EB], src[s, q].partition_broadcast(EB), sent,
                                                  S["bcb_free"][q])
                    S["bc"][b, q] = got
                    S["bc_read"].setdefault(b, []).append(got)

        def dd_spread():
            for n in range(NB * NJ):
                b, j, place = n // NJ, n % NJ, n % NSLOT
                yield from until(lambda: n < S["dd_used"] + NSLOT and b in S["dd_src"])
                for s in range(SG):
                    got = yield dd_in[place].load(sp, ddb[s * EB:(s + 1) * EB, place, :, :],
                                                  dd_dram[b % 2][j * EB:(j + 1) * EB], S["dd_src"][b], S["ddb_free"][place])
                S["dd"][b, j] = got
                S["dd_read"].setdefault(b, []).append(got)

        def scan_feed(b):
            for f in range(NF):
                for q in range(2):
                    for jj in range(NJ // NF):
                        j = f * (NJ // NF) + jj
                        place = (b * NJ + j) % NSLOT
                        yield from until(lambda: (b, j) in S["dd"] and (b, q) in S["bc"])
                        hb, fh = yield from grab(hb_ring)
                        bx_ok = yield pool.do(op("tensor_tensor", hb, ddb[:, place, 1:2, :].to_broadcast([P, 2, L]),
                                                 bcb[q][:, 0, :, :], ALU.mult), S["dd"][b, j], S["bc"][b, q], fh)
                        dA, fa = yield from grab(dA_ring)
                        for g in range(2):
                            ai = j * SG + 2 * q + g
                            dA_ok = yield act.do(op("activation", dA[:, g, :], ddb[:, place, 0, :], ACT.Exp,
                                                    scale=A_neg[:, ai:ai + 1]), S["dd"][b, j], fa, made_A)
                        if q == 1:
                            S["ddb_free"][place] = [dA_ok, bx_ok]
                            S["dd_used"] += 1
                        S["fed"].append((dA, dA_ok, hb, bx_ok))

        def mamba_scan(b):
            i = b % 2
            for f in range(NF):
                for q in range(2):
                    held = []
                    for jj in range(NJ // NF):
                        yield from until(lambda: S["fed"])
                        dA, dA_ok, hb, bx_ok = S["fed"].pop(0)
                        for g in range(2):
                            h_ok = yield dve.do(op("tensor_tensor_scan", hb[:, g, :], dA[:, g, :], hb[:, g, :], 0.0,
                                                   ALU.mult, ALU.add), dA_ok, bx_ok)
                        dA_ring.give(dA, h_ok)
                        hc_ok = yield dve.do(op("tensor_tensor", hb, hb, bcb[q][:, 1, :, :], ALU.mult), h_ok)
                        held.append((hb, hc_ok))
                    if f == NF - 1:
                        S["bcb_free"][q], S["bcb_freed"][q] = hc_ok, b
                    S["scanned"].append((b, f, q, held))

        def mamba_sum(b):
            i = b % 2
            for f in range(NF):
                for q in range(2):
                    yield from until(lambda: S["scanned"])
                    _, _, _, held = S["scanned"].pop(0)
                    y_ok = yield pe.group([op("matmul", y_pair[jj * EB:(jj + 1) * EB, f, :], sel, hb[:, g, :],
                                              start=(q == 0 and g == 0), stop=(q == 1 and g == 1))
                                           for g in range(2) for jj, (hb, _) in enumerate(held)],
                                          [m for _, m in held], S["y_free"][f], small_ready)
                    for hb, _ in held:
                        hb_ring.give(hb, y_ok)
                a = yield dve.do(op("scalar_tensor_tensor", xc[i][:, f, :], xc[i][:, f, :], col("D", f), y_pair[:, f, :],
                                    ALU.mult, ALU.add), y_ok, S["du"][b])
                S["y_free"][f] = a
                S["yT"][b] = yield dve.do(op("tensor_tensor", xc[i][:, f, :], xc[i][:, f, :], sz[i][:, f, :], ALU.mult), a)
            S["sz_free"][i] = S["yT"][b]
            S["scans"] = b + 1

        def mamba_back(b):
            i = b % 2
            ps, pf = yield from grab(banks1)
            hv = halves(ps)
            mm = yield from product([(hv[:, t, :], [(xc[i][:, k, t * P:(t + 1) * P], w_out[:, k, :]) for k in range(NF)]) for t in range(NT)],
                         S["yT"][b], pf)
            S["xc_free"][i] = mm
            S["outs"] = b + 1
            yield from until(lambda: S["back_loads"] > b)
            loaded = S["x_back"]
            x1_ok = yield dve.do(op("tensor_tensor", xh_back, hv, xh_back, ALU.add), mm, loaded)
            banks1.give(ps, x1_ok)
            h2, f2 = yield from grab(tmp_back)
            h2_ok = yield from normalise(xh_back, tok(h2), x1_ok, 1, f2)
            xb2_ok = yield pool.do(op("tensor_tensor", x_back, x_back, over_tiles(row("ffn_b2")), ALU.add), loaded)
            s_ok = yield pool.do(op("tensor_tensor", x_back, x_back, xh_back, ALU.add), x1_ok, xb2_ok)
            S["xh_back_free"] = [s_ok, h2_ok]
            ps, pf = yield from grab(banks1)
            turned = yield turn(tok(h2), h2_ok, ps, pf)
            hT, f3 = yield from grab(tmp_back)
            tmp_back.give(h2, turned)
            for f in range(NF):
                hT_ok = yield act.do(op("activation", feat(hT)[:, f, :], ps[:, f, :], ACT.Identity, scale=col("ln2_g", f),
                                                                  bias=col("ln2_b", f)), turned, f3)
            banks1.give(ps, hT_ok)
            acc, acc_free = yield from grab(banks1)
            hv2 = halves(acc)
            ps, pf = yield from grab(banks1)
            nh = HID // P
            r, fr = yield from grab(tmp_back)
            r_free, ps_free = [fr, fr], [pf, pf]

            def second(c, r_ok):
                r_free[c % 2] = yield pe.group([op("matmul", hv2[:, t, :], feat(r)[:, c % 2, t * P:(t + 1) * P], w2[:, c, :],
                                                   start=(c == 0 and t % 2 == 0), stop=(c == nh - 1), skip_group_check=True)
                                                for t in range(NT)], r_ok, acc_free)
            for c in range(nh):
                mm = yield from product([(ps[:, c % 2, :], [(w1[:, k, c * P:(c + 1) * P], feat(hT)[:, k, :]) for k in range(NF)])],
                                        hT_ok, ps_free[c % 2], ffn_ready)
                if c:
                    yield from second(c - 1, r_ok)
                r_ok = yield act.do(op("activation", feat(r)[:, c % 2, :], ps[:, c % 2, :], ACT.Relu, bias=col("ffn_b1", c)),
                                    mm, r_free[c % 2])
                ps_free[c % 2] = r_ok
            yield from second(nh - 1, r_ok)
            mm2 = r_free[1]
            banks1.give(ps, *ps_free)
            tmp_back.give(r, mm2)
            tmp_back.give(hT, mm)
            x_ok = yield dve.do(op("tensor_tensor", x_back, hv2, x_back, ALU.add), mm2, s_ok)
            banks1.give(acc, x_ok)
            sent = yield x_sent[i].load(sp, x_dram[0][b].rearrange("t p d -> p t d"), x_back, x_ok)
            S["x_sent"][b] = sent
            S["x_new"] = x_ok

        def fronts():
            for b in range(NB):
                yield from mamba_front(b)

        def middles():
            for b in range(NB):
                yield from until(lambda: b in S["z"])
                yield from mamba_middle(b)

        def feeds():
            for b in range(NB):
                yield from scan_feed(b)

        def scans():
            for b in range(NB):
                yield from mamba_scan(b)

        def sums():
            for b in range(NB):
                yield from mamba_sum(b)

        def backs():
            for b in range(NB):
                yield from until(lambda: S["scans"] > b)
                yield from mamba_back(b)
                yield from until(lambda: S["backs"] > b)

        def gates():
            for b in range(NB):
                yield from until(lambda: b in S["x_sent"])

                def give(mark):
                    S["backs"], S["x_back_free"] = b + 1, [mark, S["x_sent"][b]]
                yield from gate_step(b, x_back, S["x_new"], give, banks1, tmp_gate, state, xwo_sent, xwo_dram[0])

        weave(sums(), scans(), feeds(), bc_spread(), dd_spread(), back_loads(), x_fetches(), backs(), gates(), middles(), fronts())

        def final_state(banks):
            ps, pf = banks.take()
            hv = halves(ps)
            for t in range(NT):
                mm = pe.group([op("matmul", hv[:, t, :], c_state[:, k, t * P:(t + 1) * P], uo[:, k, :], start=k == 0,
                                  stop=k == NF - 1) for k in range(NF)], state["c"], pf).now()
            return ps, hv, mm

        ps, hv, mm = final_state(banks1)
        everything = [(x.sem, x.count) for x in (act, dve, pool, pe)] + [(a.sem, a.count) for a in
                     [*x_sent, *xwo_sent, dd_sent, *dd_in, *bc_sent, *bc_in]]

        top[0] = shared_top
        w_v = sb(NF, D)
        w_o = sb(NF, D)
        w_q = sb(NF, P)
        att_rows = sb(len(ATT_ROWS), D)
        cuo = sb(NT, D)
        x2 = [sb(NT, D) for _ in range(3)]
        qp = [sb(HU, L, dt=BF16) for _ in range(3)]
        kp = [sb(HU, L, dt=BF16) for _ in range(3)]
        parts = [sb(3, NF, L, dt=BF16) for _ in range(2)]
        v_sb = [sb(NT, NH, VW) for _ in range(2)]
        p_ring = Ring([sb(L) for _ in range(10)])
        ot = [sb(2, L) for _ in range(2)]
        on = sb(NT, HU * HD)
        oT = sb(NF, L)
        mx = [sb(HU * NT) for _ in range(2)]
        nm = sb(P)
        nm_parts = sb(3, P, dt=BF16)
        rden = sb(NT, HU)
        tmp2 = Ring([sb(NT * D) for _ in range(4)])
        tmp3 = Ring([sb(NT * D) for _ in range(5)])
        qk_rows = {"q": [0, 0, 1, 1, 0, 2], "k": [0, 1, 0, 1, 2, 0]}
        nrow = 6 * HD

        w_att.load(sp, w_v, kn(t_in["w_v"]), everything).now()
        w_att.load(sp, att_rows, t_in["att_rows"].partition_broadcast(P)).now()
        w_att.load(sp, w_o, kn(t_in["w_o"])).now()
        att_ready = w_att.load(sp, w_q, t_in["w_q"].rearrange("p (f m) -> p f m", f=NF)).now()

        cuo_ok = dve.do(op("tensor_copy", cuo, hv), mm, everything).now()
        state["c"] = start_state(mm)
        for i in range(2):
            v_set = pool.do(op("memset", v_sb[i], 0.0), everything).now()
        for i in range(2):
            v_set = pool.do(op("memset", v_sb[i][:, :, :, HD:HD + 1], 1.0), v_set).now()
        for i in range(3):
            k_ones = dve.do(op("memset", kp[i][nrow:nrow + 3], 1.0), everything).now()

        max_banks = Ring([bank(0), bank(1)])
        st_banks = Ring([bank(2), bank(3)])
        pv_banks = Ring([bank(4), bank(5)])
        banks2 = Ring([pair(3)])
        for ring in (max_banks, st_banks, pv_banks, banks2):
            ring.items = [(x, list(everything) + [cuo_ok]) for x, _ in ring.items]
        p_ring.items = [(x, everything) for x, _ in p_ring.items]
        tmp2.items = [(x, everything) for x, _ in tmp2.items]
        tmp3.items = [(x, everything) for x, _ in tmp3.items]

        x2_in, xwo_in = [arrive(f"x2_in{i}") for i in range(2)], [arrive(f"xwo_in{i}") for i in range(2)]
        part_sent = [arrive(f"part_sent{i}") for i in range(2)]
        qk_in = [arrive(f"qk_in{i}") for i in range(3)]
        nm_sent, nm_in = arrive("max_sent"), [arrive(f"max_in{i}") for i in range(3)]
        x3_sent = [arrive(f"x3_sent{i}") for i in range(2)]
        xwo2_sent = [arrive(f"xwo2_sent{i}") for i in range(2)]
        state["sent"] = []
        T = {"x2": {}, "x2_free": [everything] * 3, "parts_free": [everything, everything], "v": {}, "v_free": [everything] * 2,
             "qk_free": [everything] * 3, "qk": {}, "part": {}, "part_read": {}, "nm": {}, "nm_free": everything,
             "nm_read": {}, "ot_free": [everything] * 2, "on_free": everything, "oT_free": everything, "mx_free": [everything] * 2,
             "x3": {}, "x_sent": {}, "rden_free": everything,
             "v_used": 0, "scored": [], "shifted": [], "weights": [], "ots": [], "exps": 0, "gates": 0, "ends": 0}
        NU = 2 * NB

        def attend_front(b):
            i, i3 = b % 2, b % 3
            xs, fs = yield from grab(tmp2)
            xw, fw = yield from grab(tmp2)
            xs_ok = yield x2_in[i].load(sp, tok(xs), x_dram[0][b].rearrange("t p d -> p t d"), fs)
            xw_ok = yield xwo_in[i].load(sp, tok(xw), xwo_dram[0][b].rearrange("t p d -> p t d"), fw)
            a = yield pool.do(op("tensor_tensor", tok(xw), tok(xw), cuo, ALU.add), xw_ok, cuo_ok)
            a = yield act.do(op("activation", xw, xw, ACT.Tanh), a)
            x2_ok = yield pool.do(op("tensor_tensor", x2[i3], tok(xs), tok(xw), ALU.add), a, xs_ok, T["x2_free"][i3])
            tmp2.give(xs, x2_ok)
            tmp2.give(xw, x2_ok)
            xa, fa = yield from grab(tmp2)
            xa_ok = yield from normalise(x2[i3], tok(xa), x2_ok, 0, fa)
            T["x2"][b] = yield pool.do(op("tensor_tensor", x2[i3], x2[i3], over_tiles(att_rows[:, 1, :]), ALU.add), xa_ok, att_ready)
            ps, pf = yield from grab(banks2)
            turned = yield turn(tok(xa), xa_ok, ps, pf)
            tmp2.give(xa, turned)
            xaT, fx = yield from grab(tmp2)
            k_ok = yield dve.do(op("tensor_copy", feat(xaT), ps), turned, fx)
            banks2.give(ps, k_ok)
            ps, pf = yield from grab(banks2)
            mm = yield from product([(ps[:, f, :], [(w_q[:, f, :], feat(xaT)[:, f, :])]) for f in range(NF)], k_ok, pf, att_ready)
            q, fq = yield from grab(tmp2)
            q_ok = yield act.do(op("activation", feat(q), ps, ACT.Copy), mm, fq)
            banks2.give(ps, q_ok)
            ps, pf = yield from grab(banks2)
            hv = halves(ps)
            mm = yield from product([(hv[:, t, :], [(feat(xaT)[:, k, t * P:(t + 1) * P], w_v[:, k, :]) for k in range(NF)]) for t in range(NT)],
                         k_ok, pf)
            for t in range(NT):
                v_ok = yield dve.do(op("tensor_tensor", v_sb[i][:, t, :, 0:HD], hv[:, t, :].rearrange("p (h e) -> p h e", e=HD),
                              att_rows[:, 0, :].rearrange("p (h e) -> p h e", e=HD), ALU.add), mm, att_ready, v_set, T["v_free"][i])
            T["v"][b] = v_ok
            banks2.give(ps, v_ok)
            for n, (src, ok) in enumerate([(q, q_ok), (xaT, k_ok)]):
                pt = parts[n]
                r, fr = yield from grab(tmp2)
                a = yield dve.do(op("tensor_copy", pt[:, 0, :, :], feat(src)), ok, T["parts_free"][n])
                a = yield pool.do(op("tensor_tensor", feat(r), feat(src), pt[:, 0, :, :], ALU.subtract), a, fr)
                a = yield dve.do(op("tensor_copy", pt[:, 1, :, :], feat(r)), a)
                a = yield pool.do(op("tensor_tensor", pt[:, 2, :, :], feat(r), pt[:, 1, :, :], ALU.subtract), a)
                tmp2.give(r, a)
                tmp2.give(src, a, mm)
                sent = None
                for c in range(3):
                    sent = yield part_sent[i].load(sp, part_dram[i][n, c].rearrange("(f p) t -> p f t", p=P), pt[:, c], a, T["part_read"].get(b - 2))
                T["parts_free"][n] = sent
            T["part"][b] = sent

        def fetches():
            for u in range(NU):
                yield from until(lambda: u // 2 in T["part"] and u < T["exps"] + 3)
                b, f, s = u // 2, u % 2, u % 3
                for n, (name, dst) in enumerate([("q", qp[s]), ("k", kp[s])]):
                    for r, c in enumerate(qk_rows[name]):
                        got = yield qk_in[s].load(sp, dst[r * HD:(r + 1) * HD],
                                                  part_dram[b % 2][n, c, f * P:(f + 1) * P, :].rearrange("(h e) t -> e h t", e=HD),
                                                  T["part"][b], T["qk_free"][s])
                T["qk"][u] = got
                if f == 1:
                    T["part_read"][b] = [T["qk"][u - 1], got]

        def attend_scores(u):
            s = u % 3
            for h in range(HU):
                for t in range(NT):
                    ps, pf = yield from grab(max_banks)
                    mm = yield from product([(ps, [(qp[s][0:nrow, h, t * P:(t + 1) * P], kp[s][0:nrow, h, :])])], T["qk"][u], pf)
                    T["scored"].append((ps, mm))

        def attend_max(u):
            s, m = u % 3, mx[u % 2]
            for n in range(HU * NT):
                yield from until(lambda: T["scored"])
                ps, mm = T["scored"].pop(0)
                m_ok = yield dve.do(op("tensor_reduce", m[:, n:n + 1], ps, AXIS.X, ALU.max), mm, T["mx_free"][u % 2])
                max_banks.give(ps, m_ok)
            ps, pf = yield from grab(max_banks)
            n = HU * NT
            turned = yield pe.do(op("transpose", ps[0:n, 0:P], m, ident), m_ok, pf)
            T["mx_free"][u % 2] = turned
            a = yield dve.do(op("tensor_scalar", nm[0:n, :], ps[0:n, 0:P], -1.0, None, ALU.mult), turned, T["nm_free"])
            max_banks.give(ps, a)
            for c in range(3):
                a = yield dve.do(op("tensor_copy", nm_parts[0:n, c, :], nm[0:n, :]), a, T["nm_free"])
                if c < 2:
                    a = yield dve.do(op("tensor_tensor", nm[0:n, :], nm[0:n, :], nm_parts[0:n, c, :], ALU.subtract), a)
            sent = yield nm_sent.load(sp, max_dram[u % 2].rearrange("c r t -> r c t"), nm_parts[0:n], a, T["nm_read"].get(u - 2))
            T["nm_free"] = sent
            T["nm"][u] = yield nm_in[s].load(sp, qp[s][nrow:nrow + 3, :, :], max_dram[u % 2].rearrange("c (h r) t -> c h (r t)", h=HU), sent)
            T["nm_read"][u] = T["nm"][u]

        def attend_exp(u):
            s = u % 3
            for q in range(2):
                for kt in range(NT):
                    held = []
                    for h in range(q * 4, q * 4 + 4):
                        st, sf = yield from grab(st_banks)
                        mm = yield from product([(st, [(kp[s][0:nrow + 3, h, kt * P:(kt + 1) * P], qp[s][0:nrow + 3, h, :])])],
                                                T["nm"][u], T["qk"][u], k_ones, sf)
                        T["shifted"].append((st, mm))
            T["qk_free"][s] = mm
            T["exps"] = u + 1

        def attend_exp2(u):
            for n in range(2 * NT):
                held = []
                for _ in range(4):
                    yield from until(lambda: T["shifted"])
                    st, mm = T["shifted"].pop(0)
                    pt, pf = yield from grab(p_ring)
                    p_ok = yield act.do(op("activation", pt, st, ACT.Exp, scale=HD ** -0.5), mm, pf)
                    st_banks.give(st, p_ok)
                    held.append((pt, p_ok))
                T["weights"].append(held)

        def attend_values(u):
            b, f = u // 2, u % 2
            vb, o_u = v_sb[b % 2], ot[u % 2]
            for q in range(2):
                pv, pv_free = pv_banks.take()
                for kt in range(NT):
                    yield from until(lambda: T["weights"])
                    held = T["weights"].pop(0)
                    ok = yield pe.group([op("matmul", pv[hh * VW:(hh + 1) * VW, :], vb[:, kt, f * HU + q * 4 + hh, :], pt,
                                            start=kt == 0, stop=kt == NT - 1) for hh, (pt, _) in enumerate(held)],
                                        [p_ok for _, p_ok in held], pv_free, T["v"][b])
                    for pt, _ in held:
                        p_ring.give(pt, ok)
                ot_ok = yield dve.do(op("tensor_copy", o_u[:, q, :], pv), ok, T["ot_free"][u % 2])
                pv_banks.give(pv, ot_ok)
            if f == 1:
                T["v_free"][b % 2] = ok
                T["v_used"] = b + 1
            T["ots"].append((u, ot_ok))

        def attend_end(u):
            b, f = u // 2, u % 2
            o_u = ot[u % 2]
            _, ot_ok = T["ots"].pop(0)
            ps, pf = yield from grab(banks2)
            pv4 = ps.rearrange("p b (u r) -> p (b u) r", u=NT // 2)
            turned = yield pe.group([op("transpose", pv4[:, t, q * P:(q + 1) * P], o_u[:, q, t * P:(t + 1) * P], ident)
                                     for t in range(NT) for q in range(2)], ot_ok, pf)
            T["ot_free"][u % 2] = turned
            p5 = pv4.rearrange("p t (h e) -> p t h e", e=VW)
            r_ok = yield dve.do(op("reciprocal", rden.unsqueeze(3), p5[:, :, :, HD:HD + 1]), turned, T["rden_free"])
            for t in range(NT):
                on_ok = yield dve.do(op("tensor_tensor", on[:, t, :].rearrange("p (h e) -> p h e", e=HD), p5[:, t, :, 0:HD],
                               rden[:, t, :].unsqueeze(2).to_broadcast([P, HU, HD]), ALU.mult), r_ok, T["on_free"])
            T["rden_free"] = on_ok
            banks2.give(ps, on_ok)
            ps, pf = yield from grab(banks2)
            turned = yield pe.group([op("transpose", ps[:, 0, t * P:(t + 1) * P], on[:, t, :], ident) for t in range(NT)], on_ok, pf)
            T["on_free"] = turned
            oT_ok = yield act.do(op("activation", oT[:, f, :], ps[:, 0, :], ACT.Copy), turned, T["oT_free"] if f == 0 else None)
            banks2.give(ps, oT_ok)
            if f == 0:
                T["oT_half"] = oT_ok
                return
            ps, pf = yield from grab(banks2)
            hv = halves(ps)
            mm = yield from product([(hv[:, t, :], [(oT[:, k, t * P:(t + 1) * P], w_o[:, k, :]) for k in range(NF)]) for t in range(NT)],
                         oT_ok, T["oT_half"], pf)
            T["oT_free"] = mm
            i3 = b % 3
            x3_ok = yield dve.do(op("tensor_tensor", x2[i3], hv, x2[i3], ALU.add), mm, T["x2"][b])
            banks2.give(ps, x3_ok)
            T["x3"][b] = x3_ok
            T["x_sent"][b] = yield x3_sent[b % 2].load(sp, x_dram[1][b].rearrange("t p d -> p t d"), x2[i3], x3_ok)

        def second_gate(b):
            def give(mark):
                T["x2_free"][b % 3] = [mark, T["x_sent"][b]]
            yield from gate_step(b, x2[b % 3], T["x3"][b], give, banks2, tmp3, state, xwo2_sent, xwo_dram[1])

        def attend_fronts():
            for b in range(NB):
                yield from until(lambda: T["v_used"] >= b - 1 and T["gates"] >= b - 2)
                yield from attend_front(b)

        def attend_all_scores():
            for u in range(NU):
                yield from until(lambda: u in T["qk"])
                yield from attend_scores(u)

        def attend_maxes():
            for u in range(NU):
                yield from attend_max(u)

        def attend_exps():
            for u in range(NU):
                yield from until(lambda: u in T["nm"])
                yield from attend_exp(u)

        def attend_exps2():
            for u in range(NU):
                yield from attend_exp2(u)

        def attend_all_values():
            for u in range(NU):
                yield from until(lambda: T["ends"] >= u - 1)
                yield from attend_values(u)

        def attend_ends():
            for u in range(NU):
                yield from until(lambda: T["ots"])
                yield from attend_end(u)
                T["ends"] = u + 1

        def second_gates():
            for b in range(NB):
                yield from until(lambda: b in T["x3"])
                yield from second_gate(b)
                T["gates"] = b + 1

        weave(attend_ends(), attend_all_values(), attend_exps2(), attend_exps(), second_gates(), fetches(), attend_fronts(), attend_maxes(), attend_all_scores())
        tmp2.items += tmp3.items

        ps, hv, mm = final_state(banks2)
        cuo_ok = dve.do(op("tensor_copy", cuo, hv), mm).now()
        out_sent = [arrive(f"out_sent{i}") for i in range(2)]
        x3_in, xwo2_in = [arrive(f"x3_in{i}") for i in range(2)], [arrive(f"xwo2_in{i}") for i in range(2)]
        last = []
        for b in range(NB):
            i = b % 2
            xs, fs = tmp2.take()
            xw, fw = tmp2.take()
            xs_ok = x3_in[i].load(sp, tok(xs), x_dram[1][b].rearrange("t p d -> p t d"), fs, T["x_sent"][b]).now()
            xw_ok = xwo2_in[i].load(sp, tok(xw), xwo_dram[1][b].rearrange("t p d -> p t d"), fw, state["sent"][b]).now()
            a = (dve if b % 2 else pool).do(op("tensor_tensor", tok(xw), tok(xw), cuo, ALU.add), xw_ok, cuo_ok).now()
            a = act.do(op("activation", xw, xw, ACT.Tanh), a).now()
            a = dve.do(op("tensor_tensor", xs, xs, xw, ALU.add), a, xs_ok).now()
            sent = out_sent[i].load(sp, out[b].rearrange("(t p) d -> p t d", p=P), tok(xs), a).now()
            tmp2.give(xs, sent)
            tmp2.give(xw, a)
            last.append(sent)
        finals = last + [(a.sem, a.count) for a in [*x3_sent, *xwo2_sent, nm_sent, *part_sent]]

        block = ctx.enter_context(nc.Block())

        @block.sync
        def _(e):
            sp.emit(e)
            for s, v in sp.waits(finals):
                e.wait_ge(s, v)

        @block.scalar
        def _(e):
            act.emit(e)

        @block.vector
        def _(e):
            dve.emit(e)

        @block.gpsimd
        def _(e):
            pool.emit(e)

        @block.tensor
        def _(e):
            pe.emit(e)


def kernel(**inputs):
    import concourse.bacc as bacc
    from concourse.bass_utils import run_bass_kernel_spmd

    z = {k: np.asarray(v) for k, v in inputs.items()}
    a = lambda n: z["L0_attn_a_" + n]
    f = lambda n: z["L0_ffn_" + n]
    g = lambda n: z["L0_attn_b_" + n]
    cols = lambda v: v.reshape(-1, P).T
    conv = a("conv_w").reshape(NF, P, TAPS).transpose(1, 0, 2).reshape(P, NF * TAPS)
    a_log = a("A_log").reshape(NJ, EB, SG, NS // SG).transpose(2, 1, 0, 3).reshape(P, NJ * NS // SG)
    vec = np.concatenate([cols(a("ln2_g")), cols(a("ln2_b")), cols(a("rms_w")), conv, cols(a("conv_b")), cols(a("dt_proj_b")),
                          cols(a("D_param")), cols(a("ffn_b1")), cols(f("bf")), cols(f("bi")), cols(f("bc")), cols(f("in_c")),
                          a_log], axis=1)
    rows = np.stack([a("ln1_g"), a("ln1_b"), a("ffn_b2"), f("bo")])
    att_rows = np.stack([g("wv_b"), g("out_b")])
    w_q = np.zeros((P, NF, P), np.float32)
    for h in range(NH):
        r = h % HU * HD
        w_q[r:r + HD, h // HU, r:r + HD] = g("w_att_val")[h]
    sel = np.tile(np.eye(EB, dtype=np.float32), (SG, 1))
    arrays = {
        "x": a("x"), "vec": vec, "ident": np.eye(P, dtype=np.float32), "sel": sel, "rows": rows, "att_rows": att_rows,
        "w_in": a("in_proj_w"), "w_xp": a("x_proj_w"), "w_dt": a("dt_proj_w"), "w_out": a("out_proj_w"),
        "w1": a("ffn_w1"), "w2": a("ffn_w2"),
        "wx": np.concatenate([f("wf").T, f("wi").T, f("wc").T], axis=1),
        "uh": np.concatenate([f("uf").T, f("ui").T, f("uc").T], axis=1),
        "wo": f("wo").T, "uo": f("uo").T, "w_v": g("wv_w").T, "w_o": g("out_w").T, "w_q": w_q.reshape(P, NF * P),
    }
    nc = bacc.Bacc("TRN2", target_bir_lowering=False, num_devices=1)
    feed, t_in = {}, {}
    for name, v in arrays.items():
        feed[f"{name}_dram"] = np.ascontiguousarray(v)
        t_in[name] = nc.dram_tensor(f"{name}_dram", v.shape, F32, kind="ExternalInput").ap()
    out = nc.dram_tensor("out_dram", (NB, L, D), F32, kind="ExternalOutput").ap()
    build(nc, t_in, out)
    r = run_bass_kernel_spmd(nc, [feed], core_ids=[0])
    return r.results[0]["out_dram"]
```

```python
import numpy as np
import concourse.bass as bass
from concourse import mybir
from contextlib import ExitStack

F32 = mybir.dt.float32
BF16 = mybir.dt.bfloat16
ALU = mybir.AluOpType
ACT = mybir.ActivationFunctionType
AXIS = mybir.AxisListType

P = 128
D = 256
NB, L = 8, 512
NT = L // P
NF = D // P
NS = 16
SG = 4
EB = P // SG
NJ = D // EB
TAPS = 4
RANK = 64
HID = 4 * D
NH, HD = 16, 16
HU = NH // 2
VW = 32
EPS = 1e-5

VEC = {}
for _n, _w in [("ln2_g", 2), ("ln2_b", 2), ("rms_w", 2), ("conv_w", 8), ("conv_b", 2), ("dt_b", 2),
               ("D", 2), ("ffn_b1", 8), ("bf", 2), ("bi", 2), ("bc", 2), ("in_c", 2), ("A_log", 32)]:
    VEC[_n] = (sum(w for _, w in VEC.values()), _w)
NVEC = sum(w for _, w in VEC.values())
ROWS = ["ln1_g", "ln1_b", "ffn_b2", "bo"]
ATT_ROWS = ["wv_b", "out_b"]


OPS = {
    "activation": lambda e: e.activation, "bn_stats": lambda e: e.bn_stats, "bn_aggr": lambda e: e.bn_aggr,
    "dma_start": lambda e: e.dma_start, "matmul": lambda e: e.matmul, "memset": lambda e: e.memset,
    "reciprocal": lambda e: e.reciprocal, "scalar_tensor_tensor": lambda e: e.scalar_tensor_tensor,
    "tensor_copy": lambda e: e.tensor_copy, "tensor_reduce": lambda e: e.tensor_reduce,
    "tensor_scalar": lambda e: e.tensor_scalar, "tensor_tensor": lambda e: e.tensor_tensor,
    "tensor_tensor_reduce": lambda e: e.tensor_tensor_reduce, "tensor_tensor_scan": lambda e: e.tensor_tensor_scan,
    "transpose": lambda e: e.transpose,
}


def marks(after):
    for mark in after:
        if isinstance(mark, list):
            yield from marks(mark)
        elif mark is not None:
            yield mark


def op(name, *operands, **modes):
    return name, operands, modes


def size(ap):
    return int(np.prod(ap.shape[1:]))


def estimate(name, operands, modes):
    if name == "transpose":
        return 120
    if name == "matmul":
        stationary, moving = operands[1], operands[2]
        columns = size(moving) * (4 if moving.dtype is F32 else 1)
        return columns / (8.0 if size(stationary) == VW and moving.dtype is F32 else 2.4) + 5
    n = size(modes["in0"] if name == "tensor_tensor_reduce" else operands[1] if name in ("tensor_reduce", "bn_stats") else operands[0])
    scalars = sum(isinstance(x, bass.AP) for x in [modes.get("bias"), modes.get("scale"), *operands[2:4]])
    from_psum = len(operands) > 1 and isinstance(operands[1], bass.AP) and operands[1].name == "psum"
    if name == "activation":
        return n / 1.2 + (51 if from_psum else 93) + 93 * scalars
    if name in ("tensor_scalar", "tensor_copy") and not scalars and not from_psum:
        return n / 1.92 + 68
    return n / 0.96 + 68


class Step:

    def __init__(self, queue, issues, after, sem, by):
        self.queue, self.issues, self.after, self.sem, self.by = queue, issues, after, sem, by

    def start(self):
        return max([self.queue.free] + [Queue.due.get(m, 0.0) for m in marks(self.after)])

    def now(self):
        q = self.queue
        need = q.waits(self.after)
        for s, v in need:
            q.passed[s] = v
        start = self.start()
        if self.sem is q or self.sem is None:
            q.free = start + sum(max(estimate(*issue) * q.slow, q.least) for issue in self.issues)
            land = q.free + 60
        else:
            _, (out, _), _ = self.issues[0]
            q.free = start + 60
            Arrival.issued = max(Arrival.issued, start) + 450
            Arrival.free = max(Arrival.free, Arrival.issued + 700) + size(out) * out.shape[0] * (2 if out.dtype is BF16 else 4) / 360
            land = Arrival.free + 1900
        for i, issue in enumerate(self.issues):
            last = i == len(self.issues) - 1
            q.steps.append((need if i == 0 else [], issue, self.sem.sem if last and self.by else None, self.by))
        if not self.by:
            return None
        self.sem.count += self.by
        Queue.due[self.sem.sem, self.sem.count] = land
        return (self.sem.sem, self.sem.count)


class Queue:

    due = {}

    def __init__(self, sem, slow=1.0, least=0.0):
        self.sem, self.count, self.passed, self.steps, self.least = sem, 0, {}, [], least
        self.free, self.slow = 0.0, slow

    def waits(self, after):
        need = {}
        for mark in marks(after):
            s, v = mark
            if v > self.passed.get(s, 0):
                need[s] = max(need.get(s, 0), v)
        return list(need.items())

    def do(self, issue, *after):
        return Step(self, [issue], after, self, 1)

    def quiet(self, issue, *after):
        return Step(self, [issue], after, None, 0)

    def group(self, issues, *after):
        return Step(self, issues, after, self, 1)

    def emit(self, eng):
        for need, issue, sem, by in self.steps:
            for s, v in need:
                eng.wait_ge(s, v)
            name, operands, modes = issue
            ins = OPS[name](eng)(*operands, **modes)
            if sem is not None:
                ins.then_inc(sem, by)


class Arrival:

    issued, free = 0.0, 0.0

    def __init__(self, sem):
        self.sem, self.count = sem, 0

    def load(self, queue, out, in_, *after):
        return Step(queue, [op("dma_start", out, in_)], after, self, 16)


class Ring:

    def __init__(self, items):
        self.items = [(x, None) for x in items]

    def take(self):
        return self.items.pop(0)

    def give(self, item, *marks):
        self.items.append((item, list(marks)))


WAIT = "wait"


def grab(ring):
    while not ring.items:
        yield WAIT
    return ring.take()


def until(there):
    while not there():
        yield WAIT


class Stream:

    def __init__(self, steps):
        self.steps, self.step, self.over = steps, WAIT, False

    def go(self, mark=None):
        try:
            self.step = self.steps.send(mark)
        except StopIteration:
            self.over = True


def weave(*streams):
    live = [Stream(g) for g in streams]
    while live:
        moved = True
        while moved:
            moved = False
            for s in live:
                if s.step is WAIT:
                    s.go()
                    moved = moved or s.step is not WAIT or s.over
            live = [s for s in live if not s.over]
        if live:
            ready = [s for s in live if s.step is not WAIT]
            assert ready, "every stream waits for another"
            s = min(ready, key=lambda x: x.step.start())
            s.go(s.step.now())
            live = [s for s in live if not s.over]


def build(nc, t_in, out):
    ctx = ExitStack()
    with ctx:
        sem = lambda name: ctx.enter_context(nc.semaphore(name))
        Queue.due, Arrival.issued, Arrival.free = {}, 0.0, 0.0
        pe, act, dve, sp = (Queue(sem(n)) for n in ("pe_done", "act_done", "dve_done", "sp_done"))
        pool = Queue(sem("pool_done"), 2.05, 950.0)
        arrive = lambda name: Arrival(sem(name))

        ARENA = 53180
        arena = ctx.enter_context(nc.sbuf_tensor("arena", [P, ARENA], F32))
        top = [0]

        def sb(*shape, dt=F32):
            n = int(np.prod(shape))
            words = n if dt is F32 else (n + 1) // 2
            at = top[0]
            top[0] += words
            assert top[0] <= ARENA, (top[0], ARENA)
            v = arena[:, at:at + words]
            if dt is not F32:
                v = v.bitcast(dt)
            if len(shape) > 1:
                names = " ".join(f"d{i}" for i in range(len(shape)))
                v = v.rearrange(f"p ({names}) -> p {names}",
                                **{f"d{i}": s for i, s in enumerate(shape)})
            return v

        psum = ctx.enter_context(nc.psum_tensor("psum", [P, 8, L], F32))
        bank = lambda i: psum[:, i, :]

        dram = lambda name, shape, dt: nc.dram_tensor(name, shape, dt, kind="Internal").ap()
        dd_dram = [dram(f"dd{i}", (D, 2, L), F32) for i in range(2)]
        bc_dram = [dram(f"bc{i}", (2 * NS, L), F32) for i in range(2)]
        xh_dram = [dram(f"xh{i}", (NT, P, D), F32) for i in range(4)]
        part_dram = [dram(f"parts{i}", (2, NF, 3, HD, HU, L), BF16) for i in range(2)]
        max_dram = [dram(f"max{i}", (3, HU * NT, P), BF16) for i in range(2)]
        x_dram = [dram(f"x_after_{n}", (NB, NT, P, D), F32) for n in ("mamba", "attention")]
        xwo_dram = [dram(f"xwo_{n}", (NB, NT, P, D), F32) for n in ("first", "second")]

        ident = sb(P)
        sel = sb(EB)
        vec = sb(NVEC)
        rows = sb(len(ROWS), D)
        wx = sb(NF, 3 * D)
        uh = sb(NF, 3 * D)
        wo = sb(NF, D)
        uo = sb(NF, D)
        half_bias = sb(4)
        conv_half = sb(10)
        A_neg = sb(NJ * SG)
        c_state = sb(NF, L)
        stats = [sb(NT, 6) for _ in range(2)]
        mv = [sb(NT, 2) for _ in range(2)]
        rstd = [sb(NT) for _ in range(2)]
        neg_half = sb(NT)
        col = lambda name, i=0: vec[:, VEC[name][0] + i:VEC[name][0] + i + 1]
        row = lambda name: rows[:, ROWS.index(name), :]
        over_tiles = lambda r: r.unsqueeze(1).to_broadcast([P, NT, D])
        shared_top = top[0]

        w_small, w_mamba, w_ffn, w_gate, w_att = (arrive(f"weights_{n}") for n in
                                                  ("small", "mamba", "ffn", "gate", "attention"))
        x_in = [arrive(f"x_in{i}") for i in range(2)]
        kn = lambda ap: ap.rearrange("(k p) n -> p k n", p=P)

        w_out = sb(NF, D)
        w1 = sb(NF, HID)
        w2 = sb(HID // P, D)
        x_back = sb(NT, D)
        xh_back = sb(NT, D)
        xc = [sb(NF, L) for _ in range(2)]
        tmp_back = Ring([sb(NT * D) for _ in range(2)])
        tmp_gate = Ring([sb(NT * D) for _ in range(3)])
        scan_top = top[0]
        w_in = sb(NF, 2 * D)
        w_xp = sb(NF, RANK + 2 * NS)
        w_dt = sb(D)
        x_front = sb(NT, D)
        xi_pad = sb(NF, TAPS - 1 + L)
        sz = [sb(NF, L) for _ in range(2)]
        dbc = sb(L)
        dd_out = sb(NF, 2, L)
        NSLOT = 6
        ddb = sb(NSLOT, 2, L)
        bcb = [sb(2, 2, L) for _ in range(2)]
        dA_ring = Ring([sb(2, L) for _ in range(2)])
        hb_ring = Ring([sb(2, L) for _ in range(8)])
        tmp = Ring([sb(NT * D) for _ in range(2)])
        tmp_middle = Ring([sb(NT * D) for _ in range(2)])
        top[0] = shared_top
        p_ring = Ring([sb(L) for _ in range(10)])
        ot = [sb(2, L) for _ in range(2)]
        on = sb(NT, HU * HD)
        oT = sb(NF, L)
        mx = [sb(HU * NT) for _ in range(2)]
        nm = sb(P)
        nm_parts = sb(3, P, dt=BF16)
        rden = sb(NT, HU)
        tmp3 = Ring([sb(NT * D) for _ in range(3)])
        assert top[0] <= scan_top
        top[0] = scan_top
        w_v = sb(NF, D)
        w_o = sb(NF, D)
        w_q = sb(NF, P)
        att_rows = sb(len(ATT_ROWS), D)
        cuo = sb(NT, D)
        x2 = [sb(NT, D) for _ in range(3)]
        x_ring = Ring([sb(NT * D) for _ in range(4)])
        tmp2 = Ring([sb(NT * D) for _ in range(3)])
        attention_top = top[0]
        qp = [sb(HU, L, dt=BF16) for _ in range(3)]
        kp = [sb(HU, L, dt=BF16) for _ in range(3)]
        parts = [sb(3, NF, L, dt=BF16) for _ in range(2)]
        v_sb = [sb(NT, NH, VW) for _ in range(2)]
        top[0] = attention_top
        out_x, out_xwo = ([sb(NT, D) for _ in range(NB)] for _ in range(2))

        tok = lambda v: v.rearrange("p (t d) -> p t d", t=NT)
        feat = lambda v: v.rearrange("p (f t) -> p f t", f=NF)

        load = w_small.load
        load(sp, vec, t_in["vec"]).now()
        load(sp, ident, t_in["ident"]).now()
        load_x = lambda b, *after: x_in[b % 2].load(sp, x_front, t_in["x"][b].rearrange("(t p) d -> p t d", p=P), *after)
        x_loads = {0: load_x(0).now()}
        load(sp, sel, t_in["sel"]).now()
        small_ready = load(sp, rows, t_in["rows"].partition_broadcast(P)).now()
        w_mamba.load(sp, w_in, kn(t_in["w_in"])).now()
        w_mamba.load(sp, w_xp, kn(t_in["w_xp"])).now()
        w_mamba.load(sp, w_dt[0:RANK, :], t_in["w_dt"]).now()
        mamba_ready = w_mamba.load(sp, w_out, kn(t_in["w_out"])).now()
        w_ffn.load(sp, w1, kn(t_in["w1"])).now()
        ffn_ready = w_ffn.load(sp, w2, kn(t_in["w2"])).now()
        w_gate.load(sp, wx, kn(t_in["wx"])).now()
        w_gate.load(sp, uh, kn(t_in["uh"])).now()
        w_gate.load(sp, wo, kn(t_in["wo"])).now()
        gate_ready = w_gate.load(sp, uo, kn(t_in["uo"])).now()

        c0 = VEC["bf"][0]
        made_bias = dve.do(op("tensor_scalar", half_bias, vec[:, c0:c0 + 4], 0.5, None, ALU.mult), small_ready).now()
        c1 = VEC["conv_w"][0]
        made_conv = dve.do(op("tensor_scalar", conv_half, vec[:, c1:c1 + 10], 0.5, None, ALU.mult)).now()
        c2 = VEC["A_log"][0]
        exp_A = act.do(op("activation", A_neg, vec[:, c2:c2 + NJ * SG], ACT.Exp), small_ready).now()
        made_A = dve.do(op("tensor_scalar", A_neg, A_neg, -1.0, None, ALU.mult), exp_A).now()
        minus_half = pool.do(op("memset", neg_half, -0.5)).now()
        zero_pad = pool.do(op("memset", xi_pad[:, :, 0:TAPS - 1], 0.0)).now()

        def start_state(*after):
            z = yield pool.do(op("memset", c_state, 0.0), *after)
            for f in range(NF):
                z = yield pool.do(op("tensor_scalar", c_state[:, f, :], c_state[:, f, :], col("in_c", f), None, ALU.add), z, small_ready)
            state["c"] = z

        def normalise(src, dst, ready, which, free=None):
            st, m, r = stats[which], mv[which], rstd[which]
            for t in range(NT):
                a = yield dve.do(op("bn_stats", st[:, t, :], src[:, t, :]), ready)
            for t in range(NT):
                b_ = yield dve.do(op("bn_aggr", m[:, t, :], st[:, t, :]), a)
            c = yield dve.do(op("tensor_scalar", r.unsqueeze(2), m[:, :, 1:2], EPS, None, ALU.add), b_)
            c = yield pool.do(op("tensor_tensor", r, r, neg_half, ALU.pow), c, minus_half)
            for t in range(NT):
                d_ = yield dve.do(op("tensor_scalar", dst[:, t, :], src[:, t, :], m[:, t, 0:1], r[:, t:t + 1],
                                                           ALU.subtract, ALU.mult), c, free)
            return d_

        def turn(src, f, ready, to, free):
            return pe.group([op("transpose", to[:, t * P:(t + 1) * P], src[:, t, f * P:(f + 1) * P], ident)
                             for t in range(NT)], ready, free, small_ready)

        def product(outs, *after):
            for o, terms in outs:
                for k, (l, r) in enumerate(terms):
                    issue = op("matmul", o, l, r, start=k == 0, stop=k == len(terms) - 1)
                    done = yield (pe.do if k == len(terms) - 1 else pe.quiet)(issue, *after)
            return done

        def halves(v):
            return v.rearrange("p (u d) -> p u d", u=2)

        def token_halves():
            return [slice(0, 2), slice(2, 4)]

        def token_product(ps, tiles, lhsT, rhs, *after):
            return product([(halves(ps)[:, t - tiles.start, :], [(lhsT[:, k, t * P:(t + 1) * P], rhs[:, k, :]) for k in range(NF)])
                            for t in range(tiles.start, tiles.stop)], *after)

        def gate_step(b, x_new, ready, x_give, banks, tmp, state, xwo_arrive, xwo_out):
            xr, free = yield from grab(tmp)
            xr_done = yield from normalise(x_new, tok(xr), ready, 1, free)
            x_give(xr_done)
            xrT, free = yield from grab(tmp)
            for f in range(NF):
                ps, ps_free = yield from grab(banks)
                turned = yield turn(tok(xr), f, xr_done, ps, ps_free)
                xrT_done = yield act.do(op("activation", feat(xrT)[:, f, :], ps, ACT.Copy), turned, free)
                banks.give(ps, xrT_done)
            tmp.give(xr, turned)
            xwo, free = yield from grab(tmp)
            for tiles in token_halves():
                ps, ps_free = yield from grab(banks)
                wo_done = yield from token_product(ps, tiles, feat(xrT), wo, xrT_done, ps_free, gate_ready)
                xwo_done = yield act.do(op("activation", tok(xwo)[:, tiles, :], halves(ps), ACT.Copy), wo_done, free)
                banks.give(ps, xwo_done)
            xwo_sent = yield xwo_arrive[b % 2].load(sp, xwo_out[b].rearrange("t p d -> p t d"), tok(xwo), xwo_done)
            tmp.give(xwo, xwo_sent)
            state["sent"].append(xwo_sent)
            gates = []
            for g, (fn, sc) in [(1, (ACT.Tanh, 0.5)), (2, (ACT.Tanh, 1.0)), (0, (ACT.Tanh, 0.5))]:
                gt, free = yield from grab(tmp)
                for f in range(NF):
                    ps, ps_free = yield from grab(banks)
                    w = slice(g * D + f * P, g * D + (f + 1) * P)
                    mm = yield from product([(ps, [(wx[:, k, w], feat(xrT)[:, k, :]) for k in range(NF)]
                                              + [(uh[:, k, w], c_state[:, k, :]) for k in range(NF)])],
                                            xrT_done, ps_free, gate_ready, state["c"])
                    bias = half_bias[:, 2 * g + f:2 * g + f + 1] if g < 2 else col("bc", f)
                    done = yield act.do(op("activation", feat(gt)[:, f, :], ps, fn, bias=bias, scale=sc), mm, free, made_bias)
                    banks.give(ps, done)
                gates.append((gt, done))
                if g == 2:
                    (gi, i_ok), (gc, c_ok) = gates
                    d_ = yield dve.do(op("scalar_tensor_tensor", feat(gi), feat(gi), 1.0, feat(gc), ALU.add, ALU.mult), i_ok, c_ok)
                    tmp.give(gc, d_)
            tmp.give(xrT, mm)
            gf, f_ok = gates[2]
            a = yield dve.do(op("scalar_tensor_tensor", feat(gf), feat(gf), 1.0, c_state, ALU.add, ALU.mult), f_ok, state["c"])
            s = yield dve.do(op("tensor_tensor", gf, gf, gi, ALU.add), a, d_)
            state["c"] = yield dve.do(op("tensor_scalar", c_state, feat(gf), 0.5, None, ALU.mult), s, mm)
            for gt in (gf, gi):
                tmp.give(gt, state["c"])

        y_banks = [bank(0), bank(1)]
        banks1 = Ring([bank(i) for i in range(2, 8)])
        zeros = pool.do(op("memset", c_state, 0.0)).now()
        cleared = [act.do(op("activation", x, c_state[:, 0, :], ACT.Copy), zeros).now() for x, _ in banks1.items]
        banks1.items = [(x, [m]) for (x, _), m in zip(banks1.items, cleared)]
        state = {"sent": []}
        weave(start_state(cleared))
        bc_sent, bc_in = [arrive(f"bc_out{i}") for i in range(2)], [arrive(f"bc_in{i}") for i in range(2)]
        dd_sent, dd_in = arrive("dd_out"), [arrive(f"dd_in{i}") for i in range(NSLOT)]
        x_sent = [arrive(f"x_sent{i}") for i in range(2)]
        xwo_sent = [arrive(f"xwo_sent{i}") for i in range(2)]
        S = {
            "xh": {}, "z": {}, "xi": {}, "sz": {}, "yT": {}, "du": {}, "dd": {}, "bc": {}, "x_sent": {}, "bc_src": {}, "dd_src": {},
            "dd_read": {}, "bc_read": {}, "xh_read": {},
            "y_free": [None] * NF, "xi_free": None, "dbc_free": None, "dd_out_free": None, "xc_free": [None, None],
            "sz_free": [None, None], "ddb_free": [None] * NSLOT, "bcb_free": [None, None], "x_back_free": None,
            "xh_back_free": None,
            "fed": [], "scanned": [],
            "scans": 0, "convs": 0, "bcb_freed": [-1, -1], "dd_used": 0, "backs": 0, "back_loads": 0, "outs": 0, "gates": 0,
        }
        xh_sent = [arrive(f"xh_sent{i}") for i in range(4)]
        back_in = arrive("back_in")

        def back_loads():
            for b in range(NB):
                yield from until(lambda: b in S["xh"] and S["backs"] == b)
                yield back_in.load(sp, x_back, t_in["x"][b].rearrange("(t p) d -> p t d", p=P), S["x_back_free"])
                S["x_back"] = yield back_in.load(sp, xh_back, xh_dram[b % 4].rearrange("t p d -> p t d"), S["xh"][b], S["xh_back_free"])
                S["xh_read"][b] = S["x_back"]
                S["back_loads"] = b + 1

        def x_fetches():
            for b in range(1, NB):
                yield from until(lambda: b - 1 in S["xh"])
                x_loads[b] = yield load_x(b, S["xh"][b - 1])

        def mamba_front(b):
            i = b % 2
            yield from until(lambda: b in x_loads)
            x_ok = x_loads[b]
            xn_ok = yield from normalise(x_front, x_front, x_ok, 0)
            h, f2 = yield from grab(tmp)
            h0_ok = yield from normalise(x_front, tok(h), xn_ok, 0, f2)
            front_engine = dve if b == 0 else pool
            hg_ok = yield front_engine.do(op("tensor_tensor", tok(h), tok(h), over_tiles(row("ln1_g")), ALU.mult), h0_ok, small_ready)
            h_ok = yield front_engine.do(op("tensor_tensor", tok(h), tok(h), over_tiles(row("ln1_b")), ALU.add), hg_ok)
            xh_ok = yield pool.do(op("tensor_tensor", x_front, x_front, tok(h), ALU.add), h_ok)
            S["xh"][b] = yield xh_sent[b % 4].load(sp, xh_dram[b % 4].rearrange("t p d -> p t d"), x_front, xh_ok, S["xh_read"].get(b - 4))
            mT, f3 = yield from grab(tmp)
            for t in range(NT):
                q = yield dve.do(op("tensor_tensor_reduce", out=tok(mT)[:, t, :], in0=tok(h)[:, t, :], in1=tok(h)[:, t, :],
                                    scale=1.0, scalar=0.0, op0=ALU.mult, op1=ALU.add,
                                    accum_out=rstd[0][:, t:t + 1]), h_ok, f3)
            q = yield dve.do(op("tensor_scalar", rstd[0], rstd[0], 1.0 / D, EPS, ALU.mult, ALU.add), q)
            q = yield pool.do(op("tensor_tensor", rstd[0], rstd[0], neg_half, ALU.pow), q)
            for t in range(NT):
                m_ok = yield dve.do(op("tensor_scalar", tok(h)[:, t, :], tok(h)[:, t, :], rstd[0][:, t:t + 1], None, ALU.mult),
                                    q, xh_ok)
            for f in range(NF):
                ps, pf = yield from grab(banks1)
                turned = yield turn(tok(h), f, m_ok, ps, pf)
                mT_ok = yield act.do(op("activation", feat(mT)[:, f, :], ps, ACT.Copy, scale=col("rms_w", f)), turned, q)
                banks1.give(ps, mT_ok)
            tmp.give(h, turned)
            for part in range(2):
                if part == 0:
                    yield from until(lambda: S["convs"] >= b)
                else:
                    yield from until(lambda: S["outs"] >= b - 1)
                for f in range(NF):
                    ps, pf = yield from grab(banks1)
                    mm = yield from product([(ps, [(w_in[:, k, part * D + f * P:part * D + (f + 1) * P], feat(mT)[:, k, :])
                                                   for k in range(NF)])], mT_ok, pf, mamba_ready)
                    if part == 0:
                        xi_ok = ok = yield act.do(op("activation", xi_pad[:, f, TAPS - 1:], ps, ACT.Copy), mm, S["xi_free"], zero_pad)
                    else:
                        z_ok = ok = yield act.do(op("activation", sz[i][:, f, :], ps, ACT.Copy, scale=0.5), mm, S["sz_free"][i])
                    banks1.give(ps, ok)
            tmp.give(mT, mm)
            S["z"][b], S["xi"][b] = z_ok, xi_ok

        def mamba_middle(b):
            i = b % 2
            z_ok, xi_ok = S["z"][b], S["xi"][b]
            cv, fc = yield from grab(tmp_middle)
            for f in range(NF):
                w = lambda k, f=f: conv_half[:, f * TAPS + k:f * TAPS + k + 1]
                c_ok = yield dve.do(op("tensor_scalar", feat(cv)[:, f, :], xi_pad[:, f, TAPS - 1:], w(TAPS - 1),
                                                                  conv_half[:, 8 + f:9 + f], ALU.mult, ALU.add), xi_ok, fc, made_conv)
                for k in range(TAPS - 1):
                    c_ok = yield dve.do(op("scalar_tensor_tensor", feat(cv)[:, f, :], xi_pad[:, f, k:k + L], w(k),
                                                                                  feat(cv)[:, f, :], ALU.mult, ALU.add), c_ok)
            S["xi_free"] = c_ok
            S["convs"] = b + 1
            th, tz = dd_out[:, :, 0, :], dd_out[:, :, 1, :]
            th_ok = yield act.do(op("activation", th, feat(cv), ACT.Tanh), c_ok, S["dd_out_free"])
            tz_ok = yield act.do(op("activation", tz, sz[i], ACT.Tanh), z_ok, S["dd_out_free"])
            xc_ok = yield dve.do(op("scalar_tensor_tensor", xc[i], th, 1.0, feat(cv), ALU.add, ALU.mult), th_ok, S["xc_free"][i])
            tmp_middle.give(cv, xc_ok)
            S["sz"][b] = yield dve.do(op("scalar_tensor_tensor", sz[i], tz, 1.0, sz[i], ALU.add, ALU.mult), tz_ok)
            ps, pf = yield from grab(banks1)
            nr = RANK + 2 * NS
            mm = yield from product([(ps[0:nr, :], [(w_xp[:, k, :], xc[i][:, k, :]) for k in range(NF)])], xc_ok, pf)
            dbc_ok = yield act.do(op("activation", dbc[0:nr, :], ps[0:nr, :], ACT.Copy), mm, S["dbc_free"])
            banks1.give(ps, dbc_ok)
            sent = yield bc_sent[i].load(sp, bc_dram[i], dbc[RANK:nr, :], dbc_ok, S["bc_read"].get(b - 2))
            src = bc_dram[i].rearrange("(c s q g) t -> s q c (g t)", c=2, s=SG, q=2)
            S["bc_src"][b] = (src, sent)
            v, fv = yield from grab(tmp_middle)
            for f in range(NF):
                ps, pf = yield from grab(banks1)
                mm = yield from product([(ps, [(w_dt[0:RANK, f * P:(f + 1) * P], dbc[0:RANK, :])])], dbc_ok, pf)
                v_ok = yield act.do(op("activation", feat(v)[:, f, :], ps, ACT.Identity, bias=col("dt_b", f)), mm, fv)
                banks1.give(ps, v_ok)
            S["dbc_free"] = [mm, sent]
            u, fu = yield from grab(tmp_middle)
            ln, w_ = dd_out[:, :, 0, :], dd_out[:, :, 1, :]
            a_ok = yield dve.do(op("scalar_tensor_tensor", u, v, -1.0, v, ALU.mult, ALU.min), v_ok, fu)
            u_ok = yield act.do(op("activation", u, u, ACT.Exp), a_ok)
            w_ok = yield dve.do(op("tensor_scalar", w_, feat(u), 1.0, -1.0, ALU.add, ALU.add), u_ok, S["sz"][b])
            ln_ok = yield act.do(op("activation", ln, feat(u), ACT.Ln, bias=1.0), u_ok, xc_ok)
            r_ok = yield dve.do(op("tensor_tensor", w_, feat(u), w_, ALU.subtract), w_ok)
            s_ok = yield dve.do(op("tensor_tensor", ln, ln, w_, ALU.add), r_ok, ln_ok)
            d_ok = yield dve.do(op("scalar_tensor_tensor", ln, feat(v), 0.0, ln, ALU.max, ALU.add), s_ok)
            tmp_middle.give(u, r_ok, ln_ok)
            tmp_middle.give(v, d_ok)
            S["du"][b] = du_ok = yield (dve if b == 0 else pool).do(op("tensor_tensor", dd_out[:, :, 1, :], dd_out[:, :, 0, :], xc[i], ALU.mult), d_ok)
            sent = yield dd_sent.load(sp, dd_dram[i].rearrange("(f p) c t -> p f c t", p=P), dd_out, d_ok, du_ok, S["dd_read"].get(b - 2))
            S["dd_out_free"] = sent
            S["dd_src"][b] = sent

        def bc_spread():
            for b in range(NB):
                for q in range(2):
                    yield from until(lambda: b in S["bc_src"] and S["bcb_freed"][q] == b - 1)
                    src, sent = S["bc_src"][b]
                    for c in range(2):
                        got = yield bc_in[q].load(sp, bcb[q][:, c].rearrange("p g t -> p (g t)"),
                                                  src[:, q, c].unsqueeze(1).to_broadcast([SG, EB, 2 * L]), sent, S["bcb_free"][q])
                    S["bc"][b, q] = got
                    S["bc_read"].setdefault(b, []).append(got)

        def dd_spread():
            for n in range(NB * NJ):
                b, j, place = n // NJ, n % NJ, n % NSLOT
                yield from until(lambda: n < S["dd_used"] + NSLOT and b in S["dd_src"])
                got = yield dd_in[place].load(sp, ddb[:, place, :, :],
                                              dd_dram[b % 2][j * EB:(j + 1) * EB].unsqueeze(0).to_broadcast([SG, EB, 2, L]),
                                              S["dd_src"][b], S["ddb_free"][place])
                S["dd"][b, j] = got
                S["dd_read"].setdefault(b, []).append(got)

        def scan_feed(b):
            for f in range(NF):
                for q in range(2):
                    for jj in range(NJ // NF):
                        j = f * (NJ // NF) + jj
                        place = (b * NJ + j) % NSLOT
                        yield from until(lambda: (b, j) in S["dd"] and (b, q) in S["bc"])
                        hb, fh = yield from grab(hb_ring)
                        bx_ok = yield pool.do(op("tensor_tensor", hb, ddb[:, place, 1:2, :].to_broadcast([P, 2, L]),
                                                 bcb[q][:, 0, :, :], ALU.mult), S["dd"][b, j], S["bc"][b, q], fh)
                        dA, fa = yield from grab(dA_ring)
                        for g in range(2):
                            ai = j * SG + 2 * q + g
                            dA_ok = yield act.do(op("activation", dA[:, g, :], ddb[:, place, 0, :], ACT.Exp,
                                                    scale=A_neg[:, ai:ai + 1]), S["dd"][b, j], fa, made_A)
                        if q == 1:
                            S["ddb_free"][place] = [dA_ok, bx_ok]
                            S["dd_used"] += 1
                        S["fed"].append((dA, dA_ok, hb, bx_ok))

        def mamba_scan(b):
            for f in range(NF):
                for q in range(2):
                    held = []
                    for jj in range(NJ // NF):
                        yield from until(lambda: S["fed"])
                        dA, dA_ok, hb, bx_ok = S["fed"].pop(0)
                        for g in range(2):
                            h_ok = yield dve.do(op("tensor_tensor_scan", hb[:, g, :], dA[:, g, :], hb[:, g, :], 0.0,
                                                   ALU.mult, ALU.add), dA_ok, bx_ok)
                        dA_ring.give(dA, h_ok)
                        hc_ok = yield (pool if jj == 0 and (q == 1 or b == 0) else dve).do(
                            op("tensor_tensor", hb, hb, bcb[q][:, 1, :, :], ALU.mult), h_ok)
                        held.append((hb, hc_ok))
                    if f == NF - 1:
                        S["bcb_free"][q], S["bcb_freed"][q] = [m for _, m in held], b
                    S["scanned"].append(held)

        def mamba_sum(b):
            i = b % 2
            for f in range(NF):
                for q in range(2):
                    yield from until(lambda: S["scanned"])
                    held = S["scanned"].pop(0)
                    y_ok = yield pe.group([op("matmul", y_banks[f][jj * EB:(jj + 1) * EB, :], sel, hb[:, g, :],
                                              start=(q == 0 and g == 0), stop=(q == 1 and g == 1))
                                           for g in range(2) for jj, (hb, _) in enumerate(held)],
                                          [m for _, m in held], S["y_free"][f], small_ready)
                    for hb, _ in held:
                        hb_ring.give(hb, y_ok)
                a = yield dve.do(op("scalar_tensor_tensor", xc[i][:, f, :], xc[i][:, f, :], col("D", f), y_banks[f],
                                    ALU.mult, ALU.add), y_ok, S["du"][b])
                S["y_free"][f] = a
                S["yT"][b] = yield dve.do(op("tensor_tensor", xc[i][:, f, :], xc[i][:, f, :], sz[i][:, f, :], ALU.mult), a)
            S["sz_free"][i] = S["yT"][b]
            S["scans"] = b + 1

        def mamba_back(b):
            i = b % 2
            yield from until(lambda: S["back_loads"] > b)
            loaded = S["x_back"]
            for tiles in token_halves():
                ps, pf = yield from grab(banks1)
                mm = yield from token_product(ps, tiles, xc[i], w_out, S["yT"][b], pf)
                x1_ok = yield dve.do(op("tensor_tensor", xh_back[:, tiles, :], halves(ps), xh_back[:, tiles, :], ALU.add), mm, loaded)
                banks1.give(ps, x1_ok)
            S["xc_free"][i] = mm
            S["outs"] = b + 1
            h2, f2 = yield from grab(tmp_back)
            h2_ok = yield from normalise(xh_back, tok(h2), x1_ok, 1, f2)
            xb2_ok = yield pool.do(op("tensor_tensor", x_back, x_back, over_tiles(row("ffn_b2")), ALU.add), loaded)
            s_ok = yield pool.do(op("tensor_tensor", x_back, x_back, xh_back, ALU.add), x1_ok, xb2_ok)
            S["xh_back_free"] = [s_ok, h2_ok]
            hT, f3 = yield from grab(tmp_back)
            for f in range(NF):
                ps, pf = yield from grab(banks1)
                turned = yield turn(tok(h2), f, h2_ok, ps, pf)
                hT_ok = yield act.do(op("activation", feat(hT)[:, f, :], ps, ACT.Identity, scale=col("ln2_g", f),
                                        bias=col("ln2_b", f)), turned, f3)
                banks1.give(ps, hT_ok)
            tmp_back.give(h2, turned)
            acc = []
            for _ in range(2):
                acc.append((yield from grab(banks1)))
            nh = HID // P
            r, fr = yield from grab(tmp_back)
            r_free = [fr, fr]

            def second(c, r_ok):
                for t in range(NT):
                    done = yield (pe.do if t == NT - 1 else pe.quiet)(
                        op("matmul", halves(acc[t // 2][0])[:, t % 2, :], feat(r)[:, c % 2, t * P:(t + 1) * P], w2[:, c, :],
                           start=(c == 0 and t % 2 == 0), stop=(c == nh - 1), skip_group_check=True), r_ok, acc[0][1], acc[1][1])
                r_free[c % 2] = done
            for c in range(nh):
                ps, pf = yield from grab(banks1)
                mm = yield from product([(ps, [(w1[:, k, c * P:(c + 1) * P], feat(hT)[:, k, :]) for k in range(NF)])],
                                        hT_ok, pf, ffn_ready)
                if c:
                    yield from second(c - 1, r_ok)
                r_ok = yield act.do(op("activation", feat(r)[:, c % 2, :], ps, ACT.Relu, bias=col("ffn_b1", c)), mm, r_free[c % 2])
                banks1.give(ps, r_ok)
            yield from second(nh - 1, r_ok)
            mm2 = r_free[1]
            tmp_back.give(r, mm2)
            tmp_back.give(hT, mm)
            for tiles, (ps, _) in zip(token_halves(), acc):
                x_ok = yield dve.do(op("tensor_tensor", x_back[:, tiles, :], halves(ps), x_back[:, tiles, :], ALU.add), mm2, s_ok)
                banks1.give(ps, x_ok)
            sent = yield x_sent[i].load(sp, x_dram[0][b].rearrange("t p d -> p t d"), x_back, x_ok)
            S["x_sent"][b] = sent
            S["x_new"] = x_ok

        def fronts():
            for b in range(NB):
                yield from mamba_front(b)

        def middles():
            for b in range(NB):
                yield from until(lambda: b in S["z"])
                yield from mamba_middle(b)

        def feeds():
            for b in range(NB):
                yield from scan_feed(b)

        def scans():
            for b in range(NB):
                yield from mamba_scan(b)

        def sums():
            for b in range(NB):
                yield from mamba_sum(b)

        def backs():
            for b in range(NB):
                yield from until(lambda: S["scans"] > b)
                yield from mamba_back(b)
                yield from until(lambda: S["backs"] > b)

        def gates():
            for b in range(NB):
                yield from until(lambda: b in S["x_sent"])

                def give(mark):
                    S["backs"], S["x_back_free"] = b + 1, [mark, S["x_sent"][b]]
                yield from gate_step(b, x_back, S["x_new"], give, banks1, tmp_gate, state, xwo_sent, xwo_dram[0])
                S["gates"] = b + 1

        def final_state(banks, *after):
            for tiles in token_halves():
                ps, pf = yield from grab(banks)
                mm = yield from token_product(ps, tiles, c_state, uo, state["c"], pf)
                done = yield dve.do(op("tensor_tensor", cuo[:, tiles, :], halves(ps),
                                       row("bo").unsqueeze(1).to_broadcast([P, 2, D]), ALU.add), mm, *after)
                banks.give(ps, done)
            state["cuo"], state["c_read"] = done, mm

        def first_final_state():
            yield from until(lambda: S["gates"] == NB and early)
            yield from final_state(banks1, early)

        qk_rows = {"q": [(0,), (0,), (0, 1), (1, 2)], "k": [(0, 1, 2), (0, 1), (0,)]}
        nrow = 6 * HD
        NU = 2 * NB
        x2_in, xwo_in = [arrive(f"x2_in{i}") for i in range(2)], [arrive(f"xwo_in{i}") for i in range(2)]
        part_sent = [arrive(f"part_sent{i}") for i in range(4)]
        qk_in = [arrive(f"qk_in{i}") for i in range(3)]
        nm_sent, nm_in = arrive("max_sent"), [arrive(f"max_in{i}") for i in range(3)]
        x3_sent = [arrive(f"x3_sent{i}") for i in range(2)]
        xwo2_sent = [arrive(f"xwo2_sent{i}") for i in range(2)]
        first_sent = state["sent"]
        early = []
        everything = []
        T = {
            "x_loaded": {}, "x2": {}, "v": {}, "part": {}, "qk": {}, "nm": {}, "x3": {}, "x_sent": {}, "out_loaded": {}, "ready": {},
            "part_read": {}, "nm_read": {},
            "x2_free": [early] * 3, "parts_free": [early] * 2, "v_free": [early] * 2, "qk_free": [early] * 3,
            "nm_free": everything, "ot_free": [everything] * 2, "on_free": everything, "oT_free": everything,
            "mx_free": [everything] * 2, "rden_free": everything,
            "scored": [], "shifted": [], "weights": [], "ots": [],
            "v_used": 0, "exps": 0, "gates": 0, "ends": 0,
        }

        def counts(queues, arrivals):
            return [(x.sem, x.count) for x in queues] + [(a.sem, a.count) for a in arrivals]

        def prepare():
            yield from until(lambda: S["scans"] == NB)
            early.extend(counts([act, dve, pool, pe], [*x_in, *xh_sent, dd_sent, *dd_in, *bc_sent, *bc_in]))
            yield w_att.load(sp, w_v, kn(t_in["w_v"]), early)
            yield w_att.load(sp, att_rows, t_in["att_rows"].partition_broadcast(P), early)
            yield w_att.load(sp, w_o, kn(t_in["w_o"]), early)
            T["ready"]["w"] = yield w_att.load(sp, w_q, t_in["w_q"].rearrange("p (f m) -> p f m", f=NF), early)
            for i in range(2):
                v_set = yield pool.do(op("memset", v_sb[i], 0.0), early)
                T["ready"]["v"] = yield pool.do(op("memset", v_sb[i][:, :, :, HD:HD + 1], 1.0), v_set)
            for i in range(3):
                T["ready"]["ones"] = yield dve.do(op("memset", kp[i][nrow:nrow + 3], 1.0), early)

        def x2_fetches(first, last):
            yield from until(lambda: early)
            for b in range(first, last):
                xs, fs = yield from grab(x_ring)
                xw, fw = yield from grab(x_ring)
                xs_ok = yield x2_in[b % 2].load(sp, tok(xs), x_dram[0][b].rearrange("t p d -> p t d"), fs, early, S["x_sent"][b])
                xw_ok = yield xwo_in[b % 2].load(sp, tok(xw), xwo_dram[0][b].rearrange("t p d -> p t d"), fw, early, first_sent[b])
                T["x_loaded"][b] = xs, xs_ok, xw, xw_ok

        weave(fronts(), backs(), dd_spread(), gates(), feeds(), scans(), sums(), middles(),
              x2_fetches(0, 2), first_final_state(), bc_spread(), x_fetches(), back_loads(), prepare())
        everything.extend(counts([act, dve, pool, pe], [*x_sent, *xwo_sent]))
        state["sent"] = []
        cuo_ok = state["cuo"]
        att_ready, v_set, k_ones = T["ready"]["w"], T["ready"]["v"], T["ready"]["ones"]

        max_banks, st_banks, pv_banks, banks2 = (Ring([]) for _ in range(4))
        max_banks.items = [(x, early) for x in y_banks]
        banks2.items, st_banks.items, pv_banks.items = banks1.items[0:3], banks1.items[3:5], banks1.items[5:6]
        p_ring.items = [(x, everything) for x, _ in p_ring.items]
        tmp2.items = [(x, early) for x, _ in tmp2.items]
        tmp3.items = [(x, everything) for x, _ in tmp3.items]

        def second_start():
            yield from start_state(state["c_read"])
            T["started"] = True

        def attend_front(b):
            i, i3 = b % 2, b % 3
            front_engine = dve if b == 0 else pool
            yield from until(lambda: b in T["x_loaded"])
            xs, xs_ok, xw, xw_ok = T["x_loaded"][b]
            a = yield front_engine.do(op("tensor_tensor", tok(xw), tok(xw), cuo, ALU.add), xw_ok, cuo_ok)
            a = yield act.do(op("activation", xw, xw, ACT.Tanh), a)
            x2_ok = yield front_engine.do(op("tensor_tensor", x2[i3], tok(xs), tok(xw), ALU.add), a, xs_ok, T["x2_free"][i3])
            x_ring.give(xs, x2_ok)
            x_ring.give(xw, x2_ok)
            xa, fa = yield from grab(tmp2)
            xa_ok = yield from normalise(x2[i3], tok(xa), x2_ok, 0, fa)
            T["x2"][b] = yield pool.do(op("tensor_tensor", x2[i3], x2[i3], over_tiles(att_rows[:, 1, :]), ALU.add), xa_ok, att_ready)
            xaT, fx = yield from grab(tmp2)
            for f in range(NF):
                ps, pf = yield from grab(banks2)
                turned = yield turn(tok(xa), f, xa_ok, ps, pf)
                k_ok = yield dve.do(op("tensor_copy", feat(xaT)[:, f, :], ps), turned, fx)
                banks2.give(ps, k_ok)
            tmp2.give(xa, turned)
            q, fq = yield from grab(tmp2)
            for f in range(NF):
                ps, pf = yield from grab(banks2)
                mm = yield from product([(ps, [(w_q[:, f, :], feat(xaT)[:, f, :])])], k_ok, pf, att_ready)
                q_ok = yield act.do(op("activation", feat(q)[:, f, :], ps, ACT.Copy), mm, fq)
                banks2.give(ps, q_ok)
            for n, src, ok in [(1, xaT, k_ok), (0, q, q_ok)]:
                pt = parts[n]

                def send(c, ok):
                    for f in range(NF):
                        sent = yield part_sent[2 * n + i].load(sp, part_dram[i][n, f, c].rearrange("e h t -> h e t"), pt[:, c, f],
                                                               ok, T["part_read"].get(b - 2))
                    return sent
                r, fr = yield from grab(tmp2)
                a = yield dve.do(op("tensor_copy", pt[:, 0, :, :], feat(src)), ok, T["parts_free"][n])
                yield from send(0, a)
                a = yield front_engine.do(op("tensor_tensor", feat(r), feat(src), pt[:, 0, :, :], ALU.subtract), a, fr)
                a = yield dve.do(op("tensor_copy", pt[:, 1, :, :], feat(r)), a)
                yield from send(1, a)
                a = yield front_engine.do(op("tensor_tensor", pt[:, 2, :, :], feat(r), pt[:, 1, :, :], ALU.subtract), a)
                T["parts_free"][n] = yield from send(2, a)
                tmp2.give(r, a)
            tmp2.give(q, a)
            T["part"][b] = list(T["parts_free"])
            for tiles in token_halves():
                ps, pf = yield from grab(banks2)
                mm = yield from token_product(ps, tiles, feat(xaT), w_v, k_ok, pf)
                for t in range(tiles.start, tiles.stop):
                    v_ok = yield dve.do(op("tensor_tensor", v_sb[i][:, t, :, 0:HD],
                                           halves(ps)[:, t - tiles.start, :].rearrange("p (h e) -> p h e", e=HD),
                                           att_rows[:, 0, :].rearrange("p (h e) -> p h e", e=HD), ALU.add),
                                        mm, att_ready, v_set, T["v_free"][i])
                banks2.give(ps, v_ok)
            T["v"][b] = v_ok
            tmp2.give(xaT, a, mm)

        def fetches():
            for u in range(NU):
                yield from until(lambda: u // 2 in T["part"] and u < T["exps"] + 3)
                b, f, s = u // 2, u % 2, u % 3
                for n, (name, dst) in enumerate([("q", qp[s]), ("k", kp[s])]):
                    r = 0
                    for cs in qk_rows[name]:
                        block = slice(r, r + len(cs) * HD)
                        got = yield qk_in[s].load(
                            sp, dst[block], part_dram[b % 2][n, f, cs[0]:cs[-1] + 1].rearrange("c e h t -> (c e) h t"),
                            T["part"][b], T["qk_free"][s])
                        r = block.stop
                T["qk"][u] = got
                if f == 1:
                    T["part_read"][b] = [T["qk"][u - 1], got]

        def attend_scores(u):
            s = u % 3
            for h in range(HU):
                for t in range(NT):
                    ps, pf = yield from grab(max_banks)
                    mm = yield from product([(ps, [(qp[s][0:nrow, h, t * P:(t + 1) * P], kp[s][0:nrow, h, :])])], T["qk"][u], pf)
                    T["scored"].append((ps, mm))

        def attend_max(u):
            s, m = u % 3, mx[u % 2]
            for n in range(HU * NT):
                yield from until(lambda: T["scored"])
                ps, mm = T["scored"].pop(0)
                m_ok = yield dve.do(op("tensor_reduce", m[:, n:n + 1], ps, AXIS.X, ALU.max), mm, T["mx_free"][u % 2])
                max_banks.give(ps, m_ok)
            ps, pf = yield from grab(max_banks)
            n = HU * NT
            turned = yield pe.do(op("transpose", ps[0:n, 0:P], m, ident), m_ok, pf)
            T["mx_free"][u % 2] = turned
            a = yield dve.do(op("tensor_scalar", nm[0:n, :], ps[0:n, 0:P], -1.0, None, ALU.mult), turned, T["nm_free"])
            max_banks.give(ps, a)
            for c in range(3):
                a = yield dve.do(op("tensor_copy", nm_parts[0:n, c, :], nm[0:n, :]), a, T["nm_free"])
                if c < 2:
                    a = yield dve.do(op("tensor_tensor", nm[0:n, :], nm[0:n, :], nm_parts[0:n, c, :], ALU.subtract), a)
            sent = yield nm_sent.load(sp, max_dram[u % 2].rearrange("c r t -> r c t"), nm_parts[0:n], a, T["nm_read"].get(u - 2))
            T["nm_free"] = sent
            T["nm"][u] = yield nm_in[s].load(sp, qp[s][nrow:nrow + 3, :, :], max_dram[u % 2].rearrange("c (h r) t -> c h (r t)", h=HU), sent)
            T["nm_read"][u] = T["nm"][u]

        def attend_shifted(u):
            s = u % 3
            for q in range(2):
                for kt in range(NT):
                    for h in range(q * 4, q * 4 + 4):
                        st, sf = yield from grab(st_banks)
                        mm = yield from product([(st, [(kp[s][0:nrow + 3, h, kt * P:(kt + 1) * P], qp[s][0:nrow + 3, h, :])])],
                                                T["nm"][u], T["qk"][u], k_ones, sf)
                        T["shifted"].append((st, mm))
            T["qk_free"][s] = mm
            T["exps"] = u + 1

        def attend_exp(u):
            for n in range(2 * NT):
                held = []
                for _ in range(4):
                    yield from until(lambda: T["shifted"])
                    st, mm = T["shifted"].pop(0)
                    pt, pf = yield from grab(p_ring)
                    p_ok = yield act.do(op("activation", pt, st, ACT.Exp, scale=HD ** -0.5), mm, pf)
                    st_banks.give(st, p_ok)
                    held.append((pt, p_ok))
                T["weights"].append(held)

        def attend_values(u):
            b, f = u // 2, u % 2
            vb, o_u = v_sb[b % 2], ot[u % 2]
            for q in range(2):
                pv, pv_free = pv_banks.take()
                for kt in range(NT):
                    yield from until(lambda: T["weights"])
                    held = T["weights"].pop(0)
                    ok = yield pe.group([op("matmul", pv[hh * VW:(hh + 1) * VW, :], vb[:, kt, f * HU + q * 4 + hh, :], pt,
                                            start=kt == 0, stop=kt == NT - 1) for hh, (pt, _) in enumerate(held)],
                                        [p_ok for _, p_ok in held], pv_free, T["v"][b])
                    for pt, _ in held:
                        p_ring.give(pt, ok)
                ot_ok = yield dve.do(op("tensor_copy", o_u[:, q, :], pv), ok, T["ot_free"][u % 2])
                pv_banks.give(pv, ot_ok)
            if f == 1:
                T["v_free"][b % 2] = ok
                T["v_used"] = b + 1
            T["ots"].append(ot_ok)

        def attend_end(u):
            b, f = u // 2, u % 2
            o_u = ot[u % 2]
            ot_ok = T["ots"].pop(0)
            for tiles in token_halves():
                ps, pf = yield from grab(banks2)
                turned = yield pe.group([op("transpose", ps[:, ((t - tiles.start) * 2 + q) * P:((t - tiles.start) * 2 + q + 1) * P],
                                            o_u[:, q, t * P:(t + 1) * P], ident)
                                         for t in range(tiles.start, tiles.stop) for q in range(2)], ot_ok, pf)
                p5 = ps.rearrange("p (t h e) -> p t h e", t=2, e=VW)
                r_ok = yield dve.do(op("reciprocal", rden[:, tiles, :].unsqueeze(3), p5[:, :, :, HD:HD + 1]), turned, T["rden_free"])
                for t in range(tiles.start, tiles.stop):
                    on_ok = yield dve.do(op("tensor_tensor", on[:, t, :].rearrange("p (h e) -> p h e", e=HD),
                                            p5[:, t - tiles.start, :, 0:HD],
                                            rden[:, t, :].unsqueeze(2).to_broadcast([P, HU, HD]), ALU.mult), r_ok, T["on_free"])
                banks2.give(ps, on_ok)
            T["ot_free"][u % 2] = turned
            T["rden_free"] = on_ok
            ps, pf = yield from grab(banks2)
            turned = yield pe.group([op("transpose", ps[:, t * P:(t + 1) * P], on[:, t, :], ident) for t in range(NT)], on_ok, pf)
            T["on_free"] = turned
            oT_ok = yield act.do(op("activation", oT[:, f, :], ps, ACT.Copy), turned, T["oT_free"] if f == 0 else None)
            banks2.give(ps, oT_ok)
            if f == 0:
                T["oT_half"] = oT_ok
                return
            i3 = b % 3
            for tiles in token_halves():
                ps, pf = yield from grab(banks2)
                mm = yield from token_product(ps, tiles, oT, w_o, oT_ok, T["oT_half"], pf)
                x3_ok = yield dve.do(op("tensor_tensor", x2[i3][:, tiles, :], halves(ps), x2[i3][:, tiles, :], ALU.add), mm, T["x2"][b])
                banks2.give(ps, x3_ok)
            T["oT_free"] = mm
            T["x3"][b] = x3_ok
            T["x_sent"][b] = yield x3_sent[b % 2].load(sp, x_dram[1][b].rearrange("t p d -> p t d"), x2[i3], x3_ok)

        def second_gate(b):
            def give(mark):
                T["x2_free"][b % 3] = [mark, T["x_sent"][b]]
            yield from gate_step(b, x2[b % 3], T["x3"][b], give, banks2, tmp3, state, xwo2_sent, xwo_dram[1])

        def attend_fronts():
            for b in range(NB):
                yield from until(lambda: T["v_used"] >= b - 1 and T["gates"] >= b - 2)
                yield from attend_front(b)

        def attend_all_scores():
            for u in range(NU):
                yield from until(lambda: u in T["qk"])
                yield from attend_scores(u)

        def attend_maxes():
            for u in range(NU):
                yield from attend_max(u)
            st_banks.items += max_banks.items

        def attend_all_shifted():
            for u in range(NU):
                yield from until(lambda: u in T["nm"])
                yield from attend_shifted(u)

        def attend_exps():
            for u in range(NU):
                yield from attend_exp(u)

        def attend_all_values():
            for u in range(NU):
                yield from until(lambda: T["ends"] >= u - 1 and u // 2 in T["v"])
                yield from attend_values(u)

        def attend_ends():
            for u in range(NU):
                yield from until(lambda: T["ots"])
                yield from attend_end(u)
                T["ends"] = u + 1

        def second_gates():
            for b in range(NB):
                yield from until(lambda: b in T["x3"] and "started" in T)
                yield from second_gate(b)
                T["gates"] = b + 1

        out_sent = [arrive(f"out_sent{i}") for i in range(2)]
        out_in = [arrive(f"out_in{i}") for i in range(NB)]

        def out_fetches():
            yield from until(lambda: T["ends"] == NU)
            over = counts([act, dve, pool, pe], [*part_sent, *qk_in, *nm_in])
            for b in range(NB):
                yield from until(lambda: len(state["sent"]) > b)
                yield out_in[b].load(sp, out_x[b], x_dram[1][b].rearrange("t p d -> p t d"), over, T["x_sent"][b])
                T["out_loaded"][b] = yield out_in[b].load(sp, out_xwo[b], xwo_dram[1][b].rearrange("t p d -> p t d"), over,
                                                          state["sent"][b])

        def out_step(b):
            loaded = T["out_loaded"][b]
            a = yield (pool if b % 3 == 2 else dve).do(op("tensor_tensor", out_xwo[b], out_xwo[b], cuo, ALU.add), loaded, state["cuo"])
            a = yield act.do(op("activation", out_xwo[b], out_xwo[b], ACT.Tanh), a)
            a = yield dve.do(op("tensor_tensor", out_x[b], out_x[b], out_xwo[b], ALU.add), a)
            yield out_sent[b % 2].load(sp, out[b].rearrange("(t p) d -> p t d", p=P), out_x[b], a)

        weave(attend_all_scores(), attend_exps(), attend_ends(), attend_fronts(), second_gates(), attend_all_shifted(), attend_maxes(),
              attend_all_values(), fetches(), second_start(), x2_fetches(2, NB), out_fetches())
        weave(final_state(banks2))
        weave(*(out_step(b) for b in range(NB)))
        finals = [(a.sem, a.count) for a in [*out_sent, *xh_sent, *x_sent, *xwo_sent, dd_sent, *bc_sent, *x3_sent, *xwo2_sent,
                                             nm_sent, *part_sent]]

        block = ctx.enter_context(nc.Block())

        @block.sync
        def _(e):
            sp.emit(e)
            for s, v in sp.waits(finals):
                e.wait_ge(s, v)

        @block.scalar
        def _(e):
            act.emit(e)

        @block.vector
        def _(e):
            dve.emit(e)

        @block.gpsimd
        def _(e):
            pool.emit(e)

        @block.tensor
        def _(e):
            pe.emit(e)


def kernel(**inputs):
    import concourse.bacc as bacc
    from concourse.bass_utils import run_bass_kernel_spmd

    z = {k: np.asarray(v) for k, v in inputs.items()}
    a = lambda n: z["L0_attn_a_" + n]
    f = lambda n: z["L0_ffn_" + n]
    g = lambda n: z["L0_attn_b_" + n]
    cols = lambda v: v.reshape(-1, P).T
    conv = a("conv_w").reshape(NF, P, TAPS).transpose(1, 0, 2).reshape(P, NF * TAPS)
    a_log = a("A_log").reshape(NJ, EB, SG, NS // SG).transpose(2, 1, 0, 3).reshape(P, NJ * NS // SG)
    vec = np.concatenate([cols(a("ln2_g")), cols(a("ln2_b")), cols(a("rms_w")), conv, cols(a("conv_b")), cols(a("dt_proj_b")),
                          cols(a("D_param")), cols(a("ffn_b1")), cols(f("bf")), cols(f("bi")), cols(f("bc")), cols(f("in_c")),
                          a_log], axis=1)
    rows = np.stack([a("ln1_g"), a("ln1_b"), a("ffn_b2"), f("bo")])
    att_rows = np.stack([g("wv_b"), g("out_b")])
    w_q = np.zeros((P, NF, P), np.float32)
    for h in range(NH):
        r = h % HU * HD
        w_q[r:r + HD, h // HU, r:r + HD] = g("w_att_val")[h]
    sel = np.tile(np.eye(EB, dtype=np.float32), (SG, 1))
    arrays = {
        "x": a("x"), "vec": vec, "ident": np.eye(P, dtype=np.float32), "sel": sel, "rows": rows, "att_rows": att_rows,
        "w_in": a("in_proj_w"), "w_xp": a("x_proj_w"), "w_dt": a("dt_proj_w"), "w_out": a("out_proj_w"),
        "w1": a("ffn_w1"), "w2": a("ffn_w2"),
        "wx": np.concatenate([f("wf").T, f("wi").T, f("wc").T], axis=1),
        "uh": np.concatenate([f("uf").T, f("ui").T, f("uc").T], axis=1),
        "wo": f("wo").T, "uo": f("uo").T, "w_v": g("wv_w").T, "w_o": g("out_w").T, "w_q": w_q.reshape(P, NF * P),
    }
    nc = bacc.Bacc("TRN2", target_bir_lowering=False, num_devices=1)
    feed, t_in = {}, {}
    for name, v in arrays.items():
        feed[f"{name}_dram"] = np.ascontiguousarray(v)
        t_in[name] = nc.dram_tensor(f"{name}_dram", v.shape, F32, kind="ExternalInput").ap()
    out = nc.dram_tensor("out_dram", (NB, L, D), F32, kind="ExternalOutput").ap()
    build(nc, t_in, out)
    r = run_bass_kernel_spmd(nc, [feed], core_ids=[0])
    return r.results[0]["out_dram"]
```
